# Optimizing a Trainium2 kernel written in Bass

```python
import numpy as np
import jax
import jax.numpy as jnp

def _softmax(x, axis=-1):
    return jax.nn.softmax(x, axis=axis)

def _gelu(x):
    return jax.nn.gelu(x, approximate=True)

def _silu(x):
    return jax.nn.silu(x)

def _sigmoid(x):
    return jax.nn.sigmoid(x)

def _layernorm(x, axis=-1, eps=1e-05):
    m = jnp.mean(x, axis=axis, keepdims=True)
    v = jnp.var(x, axis=axis, keepdims=True)
    return (x - m) / jnp.sqrt(v + eps)

def _scatter_add(tgt, idx, src, axis=0):
    return tgt.at[idx].add(src)

def _segment_sum(src, seg, n):
    return jax.ops.segment_sum(src, seg, n)
kernel_name = 'mk_seq_postln_d1_jaxref_r4_567ec6'

def setup_inputs(seed: int=0):
    np.random.seed(seed)
    _w = jnp.asarray

    def _L0_attn_setup():
        import jax, jax.numpy as jnp
        import numpy as np
        from jax import lax
        D_MODEL = 256
        D_STATE = 16
        D_CONV = 4
        EXPAND = 2
        D_INNER = EXPAND * D_MODEL
        DT_RANK = -(-D_MODEL // 16)
        B_SZ, L = (2, 128)

        def _causal_dw_conv(x_bld, w, b):
            x_bdl = jnp.transpose(x_bld, (0, 2, 1))
            y = lax.conv_general_dilated(x_bdl, w, window_strides=(1,), padding=[(D_CONV - 1, 0)], dimension_numbers=('NCW', 'OIW', 'NCW'), feature_group_count=D_INNER)
            y = y + b[None, :, None]
            return jnp.transpose(y, (0, 2, 1))

        def _selective_scan(u, dt, A, B, C, D, reverse=False):
            dA = jnp.einsum('bld,dn->bldn', dt, A)
            dB_u = jnp.einsum('bld,bld,bln->bldn', dt, u, B)
            if reverse:
                dA = jnp.flip(dA, 1)
                dB_u = jnp.flip(dB_u, 1)
            dA_shift = jnp.pad(dA[:, 1:], ((0, 0), (0, 1), (0, 0), (0, 0)))
            dA_cum = jnp.exp(jnp.flip(jnp.cumsum(jnp.flip(dA_shift, 1), 1), 1))
            xs = jnp.cumsum(dB_u * dA_cum, 1) / (dA_cum + 1e-12)
            y = jnp.einsum('bldn,bln->bld', xs, C)
            if reverse:
                y = jnp.flip(y, 1)
            return y + u * D

        def _ssm(x, res, x_proj_w, dt_proj_w, dt_proj_b, A_log, D, reverse=False):
            A = -jnp.exp(A_log)
            x_dbl = x @ x_proj_w.T
            delta, B, C = jnp.split(x_dbl, [DT_RANK, DT_RANK + D_STATE], axis=-1)
            delta = jax.nn.softplus(delta @ dt_proj_w.T + dt_proj_b)
            y = _selective_scan(x, delta, A, B, C, D, reverse=reverse)
            return y * jax.nn.silu(res)
        key = jax.random.key(seed)
        ks = jax.random.split(key, 16)
        s = 0.02
        inp = {'x': jax.random.normal(ks[0], (B_SZ, L, D_MODEL), jnp.float32), 'in_proj_w': jax.random.normal(ks[1], (2 * D_INNER, D_MODEL), jnp.float32) * s, 'conv_w': jax.random.normal(ks[2], (D_INNER, 1, D_CONV), jnp.float32) * s, 'conv_b': jnp.zeros((D_INNER,), jnp.float32), 'x_proj_w': jax.random.normal(ks[3], (DT_RANK + 2 * D_STATE, D_INNER), jnp.float32) * s, 'dt_proj_w': jax.random.normal(ks[4], (D_INNER, DT_RANK), jnp.float32) * s, 'dt_proj_b': jax.random.normal(ks[5], (D_INNER,), jnp.float32) * s, 'A_log': jnp.log(jnp.broadcast_to(jnp.arange(1, D_STATE + 1, dtype=jnp.float32), (D_INNER, D_STATE))), 'D': jnp.ones((D_INNER,), jnp.float32), 'out_proj_w': jax.random.normal(ks[6], (D_MODEL, D_INNER), jnp.float32) * s, 'conv_b_w': jax.random.normal(ks[7], (D_INNER, 1, D_CONV), jnp.float32) * s, 'conv_b_b': jnp.zeros((D_INNER,), jnp.float32), 'x_proj_b_w': jax.random.normal(ks[8], (DT_RANK + 2 * D_STATE, D_INNER), jnp.float32) * s, 'dt_proj_b_w': jax.random.normal(ks[9], (D_INNER, DT_RANK), jnp.float32) * s, 'dt_proj_b_b': jax.random.normal(ks[10], (D_INNER,), jnp.float32) * s, 'A_b_log': jnp.log(jnp.broadcast_to(jnp.arange(1, D_STATE + 1, dtype=jnp.float32), (D_INNER, D_STATE))), 'D_b': jnp.ones((D_INNER,), jnp.float32)}
        return inp
    _L0_attn_in = _L0_attn_setup()

    def _L0_ffn_setup():
        import jax, jax.numpy as jnp
        import numpy as np
        B, N, D = (4, 1024, 256)
        E, S, F = (16, 64, 512)
        DO = 256
        EPS = 1e-05

        def _layernorm(x, g, b):
            mu = jnp.mean(x, axis=-1, keepdims=True)
            var = jnp.mean(jnp.square(x - mu), axis=-1, keepdims=True)
            return (x - mu) * jax.lax.rsqrt(var + EPS) * g + b
        key = jax.random.key(seed)
        ks = jax.random.split(key, 8)
        d = {'x': jax.random.normal(ks[0], (B, N, D), dtype=jnp.float32), 'norm_g': jnp.ones((D,), jnp.float32), 'norm_b': jnp.zeros((D,), jnp.float32), 'slot_g': jnp.ones((D,), jnp.float32), 'slot_b': jnp.zeros((D,), jnp.float32), 'scale': jnp.ones((1,), jnp.float32), 'slot_embeds': jax.random.normal(ks[1], (E, S, D), jnp.float32) / np.sqrt(D), 'Wg': jax.random.normal(ks[2], (E, D, F), jnp.float32) * np.sqrt(2.0 / (D + F)), 'bg': jnp.zeros((E, F), jnp.float32), 'Wu': jax.random.normal(ks[3], (E, D, F), jnp.float32) * np.sqrt(2.0 / (D + F)), 'bu': jnp.zeros((E, F), jnp.float32), 'Wd': jax.random.normal(ks[4], (E, F, DO), jnp.float32) * np.sqrt(2.0 / (F + DO)), 'bd': jnp.zeros((E, DO), jnp.float32)}
        return d
    _L0_ffn_in = _L0_ffn_setup()
    _d = {'L0_attn_x': _L0_attn_in['x'], 'L0_attn_in_proj_w': _L0_attn_in['in_proj_w'], 'L0_attn_conv_w': _L0_attn_in['conv_w'], 'L0_attn_conv_b': _L0_attn_in['conv_b'], 'L0_attn_x_proj_w': _L0_attn_in['x_proj_w'], 'L0_attn_dt_proj_w': _L0_attn_in['dt_proj_w'], 'L0_attn_dt_proj_b': _L0_attn_in['dt_proj_b'], 'L0_attn_A_log': _L0_attn_in['A_log'], 'L0_attn_D': _L0_attn_in['D'], 'L0_attn_out_proj_w': _L0_attn_in['out_proj_w'], 'L0_attn_conv_b_w': _L0_attn_in['conv_b_w'], 'L0_attn_conv_b_b': _L0_attn_in['conv_b_b'], 'L0_attn_x_proj_b_w': _L0_attn_in['x_proj_b_w'], 'L0_attn_dt_proj_b_w': _L0_attn_in['dt_proj_b_w'], 'L0_attn_dt_proj_b_b': _L0_attn_in['dt_proj_b_b'], 'L0_attn_A_b_log': _L0_attn_in['A_b_log'], 'L0_attn_D_b': _L0_attn_in['D_b'], 'L0_ffn_norm_g': _L0_ffn_in['norm_g'], 'L0_ffn_norm_b': _L0_ffn_in['norm_b'], 'L0_ffn_slot_g': _L0_ffn_in['slot_g'], 'L0_ffn_slot_b': _L0_ffn_in['slot_b'], 'L0_ffn_scale': _L0_ffn_in['scale'], 'L0_ffn_slot_embeds': _L0_ffn_in['slot_embeds'], 'L0_ffn_Wg': _L0_ffn_in['Wg'], 'L0_ffn_bg': _L0_ffn_in['bg'], 'L0_ffn_Wu': _L0_ffn_in['Wu'], 'L0_ffn_bu': _L0_ffn_in['bu'], 'L0_ffn_Wd': _L0_ffn_in['Wd'], 'L0_ffn_bd': _L0_ffn_in['bd']}
    _x0 = _d['L0_attn_x']
    _d['L0_attn_x'] = jax.random.normal(jax.random.fold_in(jax.random.key(seed), 1), (16, 512, 256), dtype=_x0.dtype)
    del _x0
    return _d

def reference(L0_attn_x, L0_attn_in_proj_w, L0_attn_conv_w, L0_attn_conv_b, L0_attn_x_proj_w, L0_attn_dt_proj_w, L0_attn_dt_proj_b, L0_attn_A_log, L0_attn_D, L0_attn_out_proj_w, L0_attn_conv_b_w, L0_attn_conv_b_b, L0_attn_x_proj_b_w, L0_attn_dt_proj_b_w, L0_attn_dt_proj_b_b, L0_attn_A_b_log, L0_attn_D_b, L0_ffn_norm_g, L0_ffn_norm_b, L0_ffn_slot_g, L0_ffn_slot_b, L0_ffn_scale, L0_ffn_slot_embeds, L0_ffn_Wg, L0_ffn_bg, L0_ffn_Wu, L0_ffn_bu, L0_ffn_Wd, L0_ffn_bd):

    def _L0_attn_ref(x, in_proj_w, conv_w, conv_b, x_proj_w, dt_proj_w, dt_proj_b, A_log, D, out_proj_w, conv_b_w, conv_b_b, x_proj_b_w, dt_proj_b_w, dt_proj_b_b, A_b_log, D_b):
        import jax, jax.numpy as jnp
        import numpy as np
        from jax import lax
        D_MODEL = 256
        D_STATE = 16
        D_CONV = 4
        EXPAND = 2
        D_INNER = EXPAND * D_MODEL
        DT_RANK = -(-D_MODEL // 16)
        B_SZ, L = (2, 128)

        def _causal_dw_conv(x_bld, w, b):
            x_bdl = jnp.transpose(x_bld, (0, 2, 1))
            y = lax.conv_general_dilated(x_bdl, w, window_strides=(1,), padding=[(D_CONV - 1, 0)], dimension_numbers=('NCW', 'OIW', 'NCW'), feature_group_count=D_INNER)
            y = y + b[None, :, None]
            return jnp.transpose(y, (0, 2, 1))

        def _selective_scan(u, dt, A, B, C, D, reverse=False):
            dA = jnp.einsum('bld,dn->bldn', dt, A)
            dB_u = jnp.einsum('bld,bld,bln->bldn', dt, u, B)
            if reverse:
                dA = jnp.flip(dA, 1)
                dB_u = jnp.flip(dB_u, 1)
            dA_shift = jnp.pad(dA[:, 1:], ((0, 0), (0, 1), (0, 0), (0, 0)))
            dA_cum = jnp.exp(jnp.flip(jnp.cumsum(jnp.flip(dA_shift, 1), 1), 1))
            xs = jnp.cumsum(dB_u * dA_cum, 1) / (dA_cum + 1e-12)
            y = jnp.einsum('bldn,bln->bld', xs, C)
            if reverse:
                y = jnp.flip(y, 1)
            return y + u * D

        def _ssm(x, res, x_proj_w, dt_proj_w, dt_proj_b, A_log, D, reverse=False):
            A = -jnp.exp(A_log)
            x_dbl = x @ x_proj_w.T
            delta, B, C = jnp.split(x_dbl, [DT_RANK, DT_RANK + D_STATE], axis=-1)
            delta = jax.nn.softplus(delta @ dt_proj_w.T + dt_proj_b)
            y = _selective_scan(x, delta, A, B, C, D, reverse=reverse)
            return y * jax.nn.silu(res)
        xr = x @ in_proj_w.T
        xf, res = jnp.split(xr, [D_INNER], axis=-1)
        xf = jax.nn.silu(_causal_dw_conv(xf, conv_w, conv_b))
        y = _ssm(xf, res, x_proj_w, dt_proj_w, dt_proj_b, A_log, D)
        xb = jax.nn.silu(_causal_dw_conv(xf, conv_b_w, conv_b_b))
        y_b = _ssm(xb, res, x_proj_b_w, dt_proj_b_w, dt_proj_b_b, A_b_log, D_b, reverse=True)
        y = y + y_b
        return y @ out_proj_w.T

    def _L0_ffn_ref(x, norm_g, norm_b, slot_g, slot_b, scale, slot_embeds, Wg, bg, Wu, bu, Wd, bd):
        import jax, jax.numpy as jnp
        import numpy as np
        B, N, D = (4, 1024, 256)
        E, S, F = (16, 64, 512)
        DO = 256
        EPS = 1e-05

        def _layernorm(x, g, b):
            mu = jnp.mean(x, axis=-1, keepdims=True)
            var = jnp.mean(jnp.square(x - mu), axis=-1, keepdims=True)
            return (x - mu) * jax.lax.rsqrt(var + EPS) * g + b
        x = _layernorm(x, norm_g, norm_b)
        se = _layernorm(slot_embeds, slot_g, slot_b) * scale
        logits = jnp.einsum('bnd,esd->bnes', x, se)
        dispatch = jax.nn.softmax(logits, axis=1)
        combine = jax.nn.softmax(logits.reshape(x.shape[0], x.shape[1], -1), axis=-1)
        slots = jnp.einsum('bnd,bnes->besd', x, dispatch)
        gate = jax.nn.gelu(jnp.einsum('besd,edf->besf', slots, Wg) + bg[None, :, None, :], approximate=False)
        up = jnp.einsum('besd,edf->besf', slots, Wu) + bu[None, :, None, :]
        eout = jnp.einsum('besf,efo->beso', gate * up, Wd) + bd[None, :, None, :]
        eout = eout.reshape(eout.shape[0], -1, eout.shape[-1])
        return jnp.einsum('bns,bso->bno', combine, eout)
    x = L0_attn_x
    x = _layernorm(x + _L0_attn_ref(x, L0_attn_in_proj_w, L0_attn_conv_w, L0_attn_conv_b, L0_attn_x_proj_w, L0_attn_dt_proj_w, L0_attn_dt_proj_b, L0_attn_A_log, L0_attn_D, L0_attn_out_proj_w, L0_attn_conv_b_w, L0_attn_conv_b_b, L0_attn_x_proj_b_w, L0_attn_dt_proj_b_w, L0_attn_dt_proj_b_b, L0_attn_A_b_log, L0_attn_D_b), axis=-1)
    x = _layernorm(x + _L0_ffn_ref(x, L0_ffn_norm_g, L0_ffn_norm_b, L0_ffn_slot_g, L0_ffn_slot_b, L0_ffn_scale, L0_ffn_slot_embeds, L0_ffn_Wg, L0_ffn_bg, L0_ffn_Wu, L0_ffn_bu, L0_ffn_Wd, L0_ffn_bd), axis=-1)
    return x

_drawn_inputs = setup_inputs


def setup_inputs(seed=0):
    import zlib

    import numpy as np

    out = dict(_drawn_inputs(seed))
    spreads = {'L0_attn_conv_b': (0.0, 0.8),
     'L0_attn_D': (1.0, 0.6),
     'L0_attn_conv_b_b': (0.0, 0.8),
     'L0_attn_D_b': (1.0, 0.6),
     'L0_ffn_norm_g': (1.0, 0.2),
     'L0_ffn_norm_b': (0.0, 0.1),
     'L0_ffn_slot_g': (1.0, 0.2),
     'L0_ffn_slot_b': (0.0, 0.1),
     'L0_ffn_bg': (0.0, 0.1),
     'L0_ffn_bu': (0.0, 0.1),
     'L0_ffn_bd': (0.0, 0.1)}
    factors = {'L0_attn_in_proj_w': 4.321,
     'L0_attn_conv_w': 8.0,
     'L0_attn_x_proj_w': 8.0,
     'L0_attn_dt_proj_w': 8.0,
     'L0_attn_dt_proj_b': 8.0,
     'L0_attn_A_log': 8.0,
     'L0_attn_out_proj_w': 4.232,
     'L0_attn_conv_b_w': 8.0,
     'L0_attn_x_proj_b_w': 8.0,
     'L0_attn_dt_proj_b_w': 8.0,
     'L0_attn_dt_proj_b_b': 8.0,
     'L0_attn_A_b_log': 8.0}
    for name, (base, spread) in spreads.items():
        noise = np.random.default_rng([zlib.crc32(name.encode()), seed]).standard_normal(out[name].shape)
        drawn = base * np.exp(spread * noise) if base else spread * noise
        out[name] = jnp.asarray(drawn.astype(out[name].dtype))
    for name, factor in factors.items():
        out[name] = (out[name] * factor).astype(out[name].dtype)
    return out
```

```python
from contextlib import ExitStack
import math

import concourse.bass as bass
from concourse import mybir

F32 = mybir.dt.float32
I32 = mybir.dt.int32
ALU = mybir.AluOpType
ACT = mybir.ActivationFunctionType
AX_X = mybir.AxisListType.X
P = 128

LN_EPS = 1e-5
SCAN_EPS = 1e-12
HALF_NEG_LN_EPS = -0.5 * math.log(SCAN_EPS)


def halves(t):
    return t.rearrange("p a b -> p (a b)")


def make_identity(eng, ident, done):
    eng.memset(ident[:], 0.0).then_inc(done, 1)
    eng.wait_ge(done, 1)
    eng.affine_select(out=ident[:], in_=ident[:], compare_op=ALU.not_equal, fill=1.0, base=0,
                      pattern=[[-1, P]], channel_multiplier=1).then_inc(done, 1)


def mixer_stage(nc, xT, x, in_wT, conv_w, conv_b, x_wT, dt_wT, dt_b, A_log, D, out_wT, h_scr, bc_scr):
    B, L, DM = x.shape
    DI = in_wT.shape[1] // 2
    NDIR, R, _ = dt_wT.shape
    N = A_log.shape[-1]
    KC = conv_w.shape[-1]
    KM, KI, LT = DM // P, DI // P, L // P
    PAD = KC - 1
    NG = 4
    GROUPS = N // NG
    TILES = N * KI
    CREDIT = 16
    assert L == 512 and KI == 4

    USE_IN, USE_CONV, USE_X, USE_DT, USE_OUT = 0, 8, 16, 18, 26
    USES = 30
    ACT_USES = 18

    with ExitStack() as ctx:
        def sb(name, shape):
            return ctx.enter_context(nc.sbuf_tensor(name, shape, F32))

        def sem(name):
            return ctx.enter_context(nc.semaphore(name))

        work = ctx.enter_context(nc.psum_tensor("work", [P, 4, 512], F32))
        yacc = ctx.enter_context(nc.psum_tensor("yacc", [P, KI, 512], F32))

        w_in = sb("w_in", [P, KM, 2 * DI])
        w_conv = sb("w_conv", [P, NDIR, KI, KC])
        b_conv = sb("b_conv", [P, NDIR, KI])
        b_conv_half = sb("b_conv_half", [P, NDIR, KI])
        w_x = sb("w_x", [P, NDIR, KI, R + 2 * N])
        w_dt = sb("w_dt", [R, NDIR, DI])
        b_dt = sb("b_dt", [P, NDIR, KI])
        d_skip = sb("d_skip", [P, NDIR, KI])
        w_out = sb("w_out", [P, KI, DM])
        a_log = sb("a_log", [P, NDIR, KI, N])
        a_neg = sb("a_neg", [P, NDIR, KI, N])
        a_neg_half = sb("a_neg_half", [P, NDIR, KI, N])
        gate_bias = sb("gate_bias", [P, 1])
        ident = sb("ident", [P, P])
        ident_half = sb("ident_half", [P, P])
        conv_diag = sb("conv_diag", [P, NDIR, KI, KC, P])
        d_diag = sb("d_diag", [P, NDIR, KI, P])
        ones = sb("ones", [P, L])

        xT_t = sb("xT_t", [P, KM, L])
        x_t = sb("x_t", [P, LT, DM])
        xf_pad = sb("xf_pad", [P, KI, PAD + L])
        u = [sb(f"u{d}", [P, KI, PAD + L]) for d in range(NDIR)]
        res_gate = sb("res_gate", [P, KI, L])
        xdbl = sb("xdbl", [R + 2 * N, NDIR, L])
        sp_exp = sb("sp_exp", [P, NDIR * KI, L])
        sp_one = sb("sp_one", [P, NDIR * KI, L])
        dt = sb("dt", [P, NDIR * KI, L])
        tanh_a, tanh_b = sp_exp[:, 0:KI], sp_exp[:, KI:NDIR * KI]
        dtu = sp_one
        rsum = sb("rsum", [P, NDIR * KI, L])
        bc_ring = sb("bc_ring", [P, NG, 2, L])
        g_ring = sb("g_ring", [P, 4, L])
        s_ring = sb("s_ring", [P, 4, L])
        v_ring = sb("v_ring", [P, 4, L])
        yg = sb("yg", [P, KI, L])
        h_t = sb("h_t", [P, LT, DM])

        w_loaded = sem("w_loaded")
        ident_done = sem("ident_done")
        const_done = sem("const_done")
        a_exp_done = sem("a_exp_done")
        xT_loaded, x_loaded = sem("xT_loaded"), sem("x_loaded")
        mm_done, act_pre, u_done, res_done = sem("mm_done"), sem("act_pre"), sem("u_done"), sem("res_done")
        bc_stored = sem("bc_stored")
        bc_loaded = [sem(f"bc_loaded{k}") for k in range(NG)]
        z_dt_done, abs_done, exp_done, fix_done, ln_done = sem("z_dt_done"), sem("abs_done"), sem("exp_done"), sem("fix_done"), sem("ln_done")
        vec_step = sem("vec_step")
        dt_done, dtu_done, rsum_done = sem("dt_done"), sem("dtu_done"), sem("rsum_done")
        e_ready, f_ready, g_done = sem("e_ready"), sem("f_ready"), sem("g_done")
        scan_done, z_done, v_done, v_used = sem("scan_done"), sem("z_done"), sem("v_done"), sem("v_used")
        yg_done, h_done, h_stored = sem("yg_done"), sem("h_done"), sem("h_stored")
        NW = 9

        block = ctx.enter_context(nc.Block())

        @block.sync
        def _(sp):
            sp.dma_start(w_in[:], in_wT.rearrange("(k p) n -> p k n", p=P)).then_inc(w_loaded, 16)
            sp.dma_start(w_out[:], out_wT.rearrange("(k p) n -> p k n", p=P)).then_inc(w_loaded, 16)
            sp.dma_start(w_dt[:], dt_wT.rearrange("d r n -> r d n")).then_inc(w_loaded, 16)
            for dst, src in ((w_conv, conv_w), (b_conv, conv_b), (w_x, x_wT), (b_dt, dt_b), (d_skip, D), (a_log, A_log)):
                sp.dma_start(dst[:], src).then_inc(w_loaded, 16)
            sp.sem_inc(bc_stored, NDIR * 16)
            sp.sem_inc(h_stored, 16)
            with sp.Fori(0, B, 1) as b:
                sp.wait_ge(h_done, b + 1)
                sp.dma_start(xT_t[:], xT[bass.ds(b, 1)].rearrange("o (k p) l -> p (o k) l", p=P)).then_inc(xT_loaded, 16)
                sp.dma_start(x_t[:], x[bass.ds(b, 1)].rearrange("o (t p) d -> p (o t) d", p=P)).then_inc(x_loaded, 16)
                for d in range(NDIR):
                    sp.wait_ge(act_pre, b * ACT_USES + USE_X + d + 1)
                    sp.dma_start(bc_scr[bass.ds(b, 1), d].rearrange("o m l -> (o m) l"),
                                 xdbl[R:R + 2 * N, d]).then_inc(bc_stored, 16)
                for d in range(NDIR):
                    with sp.Fori(0, GROUPS, 1) as j:
                        g = sp.snap((b * NDIR + d) * GROUPS + j)
                        stored = sp.snap((b + 2) * (NDIR * 16))
                        for k in range(NG):
                            done = g * (NG * KI) + ((k + 1) * KI - NG * KI + CREDIT)
                            sp.wait_ge(g_done, done)
                            sp.wait_ge(v_done, done)
                            if k == 0:
                                sp.wait_ge(bc_stored, stored)
                            src = bc_scr[bass.ds(b, 1), d].rearrange("o (c n) l -> (o n) c l", c=2)
                            src = src[bass.ds(j * NG + k, 1)]
                            sp.dma_start(bc_ring[:, k], src.broadcast_to([P, 2, L])).then_inc(bc_loaded[k], 16)
                sp.wait_ge(h_done, b + 2)
                sp.dma_start(h_scr[bass.ds(b, 1)].rearrange("o (t p) d -> p (o t) d", p=P), h_t[:]).then_inc(h_stored, 16)
            sp.wait_ge(h_stored, (B + 1) * 16)
            sp.wait_ge(bc_stored, (B + 1) * NDIR * 16)

        @block.gpsimd
        def _(pool):
            make_identity(pool, ident, ident_done)
            pool.sem_inc(g_done, CREDIT)
            with pool.Fori(0, B, 1) as b:
                for d in range(NDIR):
                    sl = slice(d * KI, (d + 1) * KI)
                    pool.wait_ge(dt_done, b + 1)
                    pool.wait_ge(g_done, b * (NDIR * TILES) + CREDIT)
                    pool.tensor_tensor(dtu[:, sl], dt[:, sl], u[d][:, :, PAD:], ALU.mult).then_inc(dtu_done, 1)
                for d in range(NDIR):
                    with pool.Fori(0, GROUPS, 1) as j:
                        t0 = pool.snap((b * NDIR + d) * TILES + j * (NG * KI))
                        dtu_written = pool.snap((b + 1) * NDIR)
                        pool.wait_ge(dtu_done, dtu_written)
                        for k in range(NG):
                            pool.wait_ge(bc_loaded[k], t0 + 16)
                            for c in range(KI):
                                t = k * KI + c
                                pool.wait_ge(scan_done, t0 + (t - 3 + CREDIT))
                                pool.tensor_tensor(g_ring[:, c], dtu[:, d * KI + c], bc_ring[:, k, 0],
                                                   ALU.mult).then_inc(g_done, 1)

        @block.scalar
        def _(act):
            act.wait_ge(w_loaded, 16 * NW)
            act.activation(a_log[:], a_log[:], ACT.Exp).then_inc(a_exp_done, 1)
            act.wait_ge(const_done, 5)
            with act.Fori(0, B, 1) as b:
                mm0 = act.snap(b * USES)
                for m in range(KI):
                    act.wait_ge(mm_done, mm0 + (USE_IN + m + 1))
                    act.activation(xf_pad[:, m, PAD:], work[:, m], ACT.Copy).then_inc(act_pre, 1)
                for m in range(KI):
                    act.wait_ge(mm_done, mm0 + (USE_IN + KI + m + 1))
                    act.activation(res_gate[:, m], work[:, m], ACT.Copy, scale=0.5)
                    act.activation(tanh_a[:, m], work[:, m], ACT.Tanh, scale=0.5).then_inc(act_pre, 1)
                for d in range(NDIR):
                    if d == 1:
                        act.wait_ge(res_done, b + 1)
                    th = (tanh_b, tanh_a)[d]
                    for c in range(KI):
                        act.wait_ge(mm_done, mm0 + (USE_CONV + d * KI + c + 1))
                        act.activation(u[d][:, c, PAD:], work[:, c], ACT.Identity, scale=0.5,
                                       bias=b_conv_half[:, d, c:c + 1])
                        act.activation(th[:, c], work[:, c], ACT.Tanh, scale=0.5,
                                       bias=b_conv_half[:, d, c:c + 1]).then_inc(act_pre, 1)
                act.wait_ge(bc_stored, (b + 1) * (NDIR * 16))
                for d in range(NDIR):
                    act.wait_ge(mm_done, mm0 + (USE_X + d + 1))
                    act.activation(xdbl[:, d], work[0:R + 2 * N, d], ACT.Copy).then_inc(act_pre, 1)
                for d in range(NDIR):
                    for c in range(KI):
                        i = d * KI + c
                        act.wait_ge(z_dt_done, b * (NDIR * KI) + i + 1)
                        act.activation(sp_exp[:, i], dt[:, i], ACT.Abs).then_inc(abs_done, 1)
                act.wait_ge(abs_done, (b + 1) * (NDIR * KI))
                act.activation(sp_exp[:], sp_exp[:], ACT.Exp, scale=-1.0).then_inc(exp_done, 1)
                act.wait_ge(fix_done, b + 1)
                act.activation(sp_one[:], sp_one[:], ACT.Ln).then_inc(ln_done, 1)
                act.wait_ge(rsum_done, b + 1)
                for d in range(NDIR):
                    for j in range(GROUPS):
                        t0 = act.snap(b * (NDIR * TILES) + (d * TILES + j * (NG * KI)))
                        for k in range(NG):
                            for c in range(KI):
                                t = k * KI + c
                                i = d * KI + c
                                n = slice(j * NG + k, j * NG + k + 1)
                                act.wait_ge(scan_done, t0 + (t - 1 + CREDIT))
                                act.activation(work[:, t % 2], dt[:, i], ACT.Exp,
                                               scale=a_neg[:, d, c, n]).then_inc(e_ready, 1)
                                act.wait_ge(v_done, t0 + (t - 1 + CREDIT))
                                act.activation(work[:, 2 + t % 2], rsum[:, i], ACT.Tanh,
                                               scale=a_neg_half[:, d, c, n], bias=gate_bias[:]).then_inc(f_ready, 1)

        @block.vector
        def _(dve):
            dve.memset(ones[:], 1.0).then_inc(const_done, 1)
            dve.memset(gate_bias[:], HALF_NEG_LN_EPS).then_inc(const_done, 1)
            for pad in (xf_pad, u[0]):
                dve.memset(pad[:, :, 0:PAD], 0.0).then_inc(const_done, 1)
            dve.memset(rsum[:], 0.0).then_inc(vec_step, 1)
            dve.wait_ge(w_loaded, 16 * NW)
            dve.wait_ge(ident_done, 2)
            dve.tensor_scalar(ident_half[:], ident[:], 0.5, None, ALU.mult)
            dve.tensor_scalar(b_conv_half[:], b_conv[:], 0.5, None, ALU.mult)
            for d in range(NDIR):
                for c in range(KI):
                    dve.tensor_scalar(d_diag[:, d, c], ident[:], d_skip[:, d, c:c + 1], None, ALU.mult)
                    for k in range(KC):
                        dve.tensor_scalar(conv_diag[:, d, c, k], ident[:], w_conv[:, d, c, k:k + 1], None, ALU.mult)
            dve.wait_ge(a_exp_done, 1)
            dve.tensor_scalar(a_neg[:], a_log[:], -1.0, None, ALU.mult)
            dve.tensor_scalar(a_neg_half[:], a_log[:], -0.5, None, ALU.mult).then_inc(const_done, 1)
            dve.wait_ge(const_done, 5)
            dve.wait_ge(vec_step, 1)
            for s in (scan_done, z_done, v_done):
                dve.sem_inc(s, CREDIT)
            for s in (h_done, yg_done):
                dve.sem_inc(s, 1)
            STEPS = 2
            with dve.Fori(0, B, 1) as b:
                mm0 = dve.snap(b * USES)
                pre0 = dve.snap(b * ACT_USES)
                step0 = dve.snap(b * STEPS)
                dve.wait_ge(act_pre, pre0 + (USE_IN + 2 * KI))
                dve.scalar_tensor_tensor(out=res_gate[:], in0=tanh_a, scalar=1.0, in1=res_gate[:],
                                         op0=ALU.add, op1=ALU.mult).then_inc(res_done, 1)
                for d in range(NDIR):
                    dve.wait_ge(act_pre, pre0 + (USE_CONV + (d + 1) * KI))
                    dve.scalar_tensor_tensor(out=u[d][:, :, PAD:], in0=(tanh_b, tanh_a)[d], scalar=1.0,
                                             in1=u[d][:, :, PAD:], op0=ALU.add, op1=ALU.mult).then_inc(u_done, 1)
                for d in range(NDIR):
                    for c in range(KI):
                        dve.wait_ge(mm_done, mm0 + (USE_DT + d * KI + c + 1))
                        dve.tensor_scalar(dt[:, d * KI + c], work[:, c], b_dt[:, d, c:c + 1], None,
                                          ALU.add).then_inc(z_dt_done, 1)
                dve.wait_ge(exp_done, b + 1)
                dve.tensor_scalar(sp_one[:], sp_exp[:], 1.0, None, ALU.add).then_inc(vec_step, 1)
                dve.wait_ge(vec_step, step0 + 2)
                dve.scalar_tensor_tensor(out=sp_exp[:], in0=sp_one[:], scalar=1.0, in1=sp_exp[:],
                                         op0=ALU.subtract, op1=ALU.subtract).then_inc(fix_done, 1)
                dve.wait_ge(fix_done, b + 1)
                dve.scalar_tensor_tensor(out=dt[:], in0=dt[:], scalar=0.0, in1=sp_exp[:],
                                         op0=ALU.max, op1=ALU.subtract).then_inc(vec_step, 1)
                dve.wait_ge(vec_step, step0 + 3)
                dve.wait_ge(ln_done, b + 1)
                dve.tensor_tensor(dt[:], dt[:], sp_one[:], ALU.add).then_inc(dt_done, 1)
                dve.wait_ge(dt_done, b + 1)
                for d in range(NDIR):
                    for c in range(KI):
                        i = d * KI + c
                        out, src = (rsum[:, i, 0:L - 1], dt[:, i, 1:L]) if d == 0 else (rsum[:, i, 1:L], dt[:, i, 0:L - 1])
                        if d == 0:
                            out, src = out[:, ::-1], src[:, ::-1]
                        ins = dve.tensor_tensor_scan(out, ones[:, 0:L - 1], src, 0.0, ALU.mult, ALU.add)
                ins.then_inc(rsum_done, 1)
                for d in range(NDIR):
                    flip = (lambda ap: ap) if d == 0 else (lambda ap: ap[:, ::-1])
                    with dve.Fori(0, GROUPS, 1) as j:
                        t0 = dve.snap((b * NDIR + d) * TILES + j * (NG * KI))

                        def scan(t):
                            dve.wait_ge(e_ready, t0 + (t + 1))
                            dve.wait_ge(g_done, t0 + (t + 1 + CREDIT))
                            dve.tensor_tensor_scan(flip(s_ring[:, t % 4]), flip(work[:, t % 2]), flip(g_ring[:, t % 4]),
                                                   0.0, ALU.mult, ALU.add).then_inc(scan_done, 1)

                        def guard(t):
                            dve.wait_ge(f_ready, t0 + (t + 1))
                            dve.wait_ge(scan_done, t0 + (t + 1 + CREDIT))
                            dve.scalar_tensor_tensor(out=work[:, 2 + t % 2], in0=work[:, 2 + t % 2], scalar=1.0,
                                                     in1=s_ring[:, t % 4], op0=ALU.add, op1=ALU.mult).then_inc(z_done, 1)

                        def times_c(t):
                            dve.wait_ge(z_done, t0 + (t + 1 + CREDIT))
                            dve.wait_ge(v_used, t0 + (t - 3 + CREDIT))
                            dve.tensor_tensor(v_ring[:, t % 4], work[:, 2 + t % 2], flip(bc_ring[:, t // KI, 1]),
                                              ALU.mult).then_inc(v_done, 1)

                        scan(0)
                        for t in range(NG * KI):
                            guard(t)
                            if t + 1 < NG * KI:
                                scan(t + 1)
                            times_c(t)
                dve.wait_ge(v_used, (b + 1) * (NDIR * TILES) + CREDIT)
                dve.tensor_tensor(yg[:], yacc[:], res_gate[:], ALU.mult).then_inc(yg_done, 1)
                dve.wait_ge(mm_done, (b + 1) * USES)
                dve.wait_ge(x_loaded, (b + 1) * 16)
                dve.wait_ge(h_stored, (b + 1) * 16)
                dve.tensor_tensor(h_t[:], work[:, :, 0:DM], x_t[:], ALU.add).then_inc(h_done, 1)

        @block.tensor
        def _(pe):
            pe.wait_ge(w_loaded, 16 * NW)
            pe.wait_ge(const_done, 5)
            pe.sem_inc(v_used, CREDIT)
            with pe.Fori(0, B, 1) as b:
                pre0 = pe.snap(b * ACT_USES)
                pe.wait_ge(xT_loaded, (b + 1) * 16)
                for m in range(2 * KI):
                    if m < KI:
                        pe.wait_ge(h_done, b + 1)
                    else:
                        pe.wait_ge(act_pre, pre0 + (USE_IN + m - 3))
                    for k in range(KM):
                        mm = pe.matmul(work[:, m % 4], w_in[:, k, m * P:(m + 1) * P], xT_t[:, k],
                                       start=(k == 0), stop=(k == KM - 1))
                    mm.then_inc(mm_done, 1)
                for d in range(NDIR):
                    src = (xf_pad, u[0])[d]
                    if d == 1:
                        pe.wait_ge(u_done, b * NDIR + 1)
                    for c in range(KI):
                        pe.wait_ge(act_pre, pre0 + (USE_CONV + d * KI + c - 3))
                        for k in range(KC):
                            mm = pe.matmul(work[:, c], conv_diag[:, d, c, k], src[:, c, k:k + L],
                                           start=(k == 0), stop=(k == KC - 1))
                        mm.then_inc(mm_done, 1)
                for d in range(NDIR):
                    pe.wait_ge(u_done, b * NDIR + d + 1)
                    pe.wait_ge(act_pre, pre0 + (USE_X + d - 3))
                    for c in range(KI):
                        mm = pe.matmul(work[0:R + 2 * N, d], w_x[:, d, c], u[d][:, c, PAD:],
                                       start=(c == 0), stop=(c == KI - 1))
                    mm.then_inc(mm_done, 1)
                pe.wait_ge(yg_done, b + 1)
                for c in range(KI):
                    for d in range(NDIR):
                        pe.matmul(yacc[:, c], d_diag[:, d, c], u[d][:, c, PAD:], start=(d == 0), stop=(d == NDIR - 1),
                                  skip_group_check=True)
                for d in range(NDIR):
                    for c in range(KI):
                        if d == 0:
                            pe.wait_ge(act_pre, pre0 + USE_DT)
                        else:
                            pe.wait_ge(z_dt_done, b * (NDIR * KI) + c + 1)
                        mm = pe.matmul(work[:, c], w_dt[:, d, c * P:(c + 1) * P], xdbl[0:R, d], start=True, stop=True)
                        mm.then_inc(mm_done, 1)
                for d in range(NDIR):
                    with pe.Fori(0, GROUPS, 1) as j:
                        t0 = pe.snap((b * NDIR + d) * TILES + j * (NG * KI))
                        for t in range(NG * KI):
                            pe.wait_ge(v_done, t0 + (t + 1 + CREDIT))
                            pe.matmul(yacc[:, t % KI], ident_half[:], v_ring[:, t % 4], start=False, stop=True,
                                      skip_group_check=True).then_inc(v_used, 1)
                pe.wait_ge(yg_done, b + 2)
                for t in range(LT):
                    for c in range(KI):
                        mm = pe.matmul(work[:, t, 0:DM], yg[:, c, t * P:(t + 1) * P], w_out[:, c],
                                       start=(c == 0), stop=(c == KI - 1))
                    mm.then_inc(mm_done, 1)


def rstd_steps(dve, link, var, y, t, eps):
    link(dve.tensor_scalar(var, var, eps, None, ALU.add))
    link(dve.tensor_scalar(t.bitcast(I32), var.bitcast(I32), 1, None, ALU.arith_shift_right))
    link(dve.tensor_scalar(y.bitcast(I32), t.bitcast(I32), -1.0, float(0x5F3759DF), ALU.mult, ALU.add))
    for _ in range(4):
        link(dve.tensor_tensor(t, y, y, ALU.mult))
        link(dve.tensor_tensor(t, t, var, ALU.mult))
        link(dve.tensor_scalar(t, t, -0.5, 1.5, ALU.mult, ALU.add))
        link(dve.tensor_tensor(y, y, t, ALU.mult))


NORM_LINKS = 2 + 3 + 4 * 4


def norm_steps(dve, link, src, dst, stats, mv, rstd, tmp, done):
    rows = src.shape[1]
    for t in range(rows):
        ins = dve.bn_stats(stats[:, t], src[:, t])
    link(ins)
    dve.memset(tmp[:], 0.0)
    for t in range(rows):
        ins = dve.bn_aggr(mv[:, t], stats[:, t])
    link(ins)
    rstd_steps(dve, link, mv[:, :, 1], rstd[:], tmp[:], LN_EPS)
    for t in range(rows):
        ins = dve.tensor_scalar(dst[:, t], src[:, t], mv[:, t, 0:1], rstd[:, t:t + 1], ALU.subtract, ALU.mult)
    ins.then_inc(done, 1)


def route_stage(nc, h_scr, slot_e, slot_g, slot_b, scale, norm_g, norm_b, x1_scr, pT_scr, rinv_scr, sT_scr):
    B, L, DM = h_scr.shape
    S = slot_e.shape[0]
    E, KM = sT_scr.shape[:2]
    SE = S // E
    LT, ST = L // P, S // P
    HALF = 512
    SH = S // HALF
    TRS = KM + 2 * ST
    USE_X, USE_E, USE_P = 0, KM, KM + 1
    assert L == HALF and KM == 2

    with ExitStack() as ctx:
        def sb(name, shape):
            return ctx.enter_context(nc.sbuf_tensor(name, shape, F32))

        def sem(name):
            return ctx.enter_context(nc.semaphore(name))

        trans = ctx.enter_context(nc.psum_tensor("r_trans", [P, 2, HALF], F32))
        rows_ps = ctx.enter_context(nc.psum_tensor("r_rows", [P, 2, S], F32))
        cols_ps = ctx.enter_context(nc.psum_tensor("r_cols", [P, 2, HALF], F32))

        ident = sb("r_ident", [P, P])
        g_bc, b_bc = sb("r_g", [P, DM]), sb("r_b", [P, DM])
        sg_bc, sb_bc = sb("r_sg", [P, DM]), sb("r_sb", [P, DM])
        scale_bc = sb("r_scale", [P, 1])
        se = sb("r_se", [P, ST, DM])
        se_stats, se_mv = sb("r_se_stats", [P, ST, 6]), sb("r_se_mv", [P, ST, 2])
        se_rstd, se_tmp = sb("r_se_rstd", [P, ST]), sb("r_se_tmp", [P, ST])
        seT = sb("r_seT", [P, KM, S])
        h_t = sb("r_h", [P, LT, DM])
        stats, mv = sb("r_stats", [P, LT, 6]), sb("r_mv", [P, LT, 2])
        rstd, tmp = sb("r_rstd", [P, LT]), sb("r_tmp", [P, LT])
        x1 = sb("r_x1", [P, LT, DM])
        xn = sb("r_xn", [P, LT, DM])
        xnT = sb("r_xnT", [P, KM, L])
        row_max, row_sum, row_inv = sb("r_row_max", [P, LT]), sb("r_row_sum", [P, LT]), sb("r_row_inv", [P, LT])
        prob = sb("r_prob", [P, LT, S])
        pT = sb("r_pT", [P, ST, L])
        col_max, col_sum, col_inv = sb("r_col_max", [P, ST]), sb("r_col_sum", [P, ST]), sb("r_col_inv", [P, ST])
        disp = sb("r_disp", [P, 4, L])
        dispT = sb("r_dispT", [P, LT, S])
        sT = sb("r_sT", [P, KM, S])

        ident_done, c_loaded, se_done, seT_ps, seT_done = (sem(f"r_{n}") for n in ("ident_done", "c_loaded", "se_done", "seT_ps", "seT_done"))
        h_loaded, x1_done, xn_done, xnT_done = (sem(f"r_{n}") for n in ("h_loaded", "x1_done", "xn_done", "xnT_done"))
        tr_done, tr_act, tr_dve = sem("r_tr_done"), sem("r_tr_act"), sem("r_tr_dve")
        rows_done, rmax_done, prob_done, rinv_done = (sem(f"r_{n}") for n in ("rows_done", "rmax_done", "prob_done", "rinv_done"))
        cols_done, cmax_done, exp_done, disp_done = (sem(f"r_{n}") for n in ("cols_done", "cmax_done", "exp_done", "disp_done"))
        slot_done, sT_done = sem("r_slot_done"), sem("r_sT_done")
        x1_stored, pT_stored, rinv_stored, sT_stored = (sem(f"r_{n}") for n in ("x1_stored", "pT_stored", "rinv_stored", "sT_stored"))
        chain, cinv_done, se_normed, xn_normed = (sem(f"r_{n}") for n in ("chain", "cinv_done", "se_normed", "xn_normed"))

        block = ctx.enter_context(nc.Block())

        @block.gpsimd
        def _(pool):
            make_identity(pool, ident, ident_done)

        @block.sync
        def _(sp):
            for dst, src in ((g_bc, norm_g), (b_bc, norm_b), (sg_bc, slot_g), (sb_bc, slot_b), (scale_bc, scale)):
                sp.dma_start(dst[:], src.rearrange("(o n) -> o n", o=1).broadcast_to([P, src.shape[0]])).then_inc(c_loaded, 16)
            sp.dma_start(se[:], slot_e.rearrange("(t p) d -> p t d", p=P)).then_inc(c_loaded, 16)
            stores = ((x1_stored, 1), (rinv_stored, 1), (pT_stored, 1), (sT_stored, KM))
            for s, n in stores:
                sp.sem_inc(s, n * 16)
            with sp.Fori(0, B, 1) as b:
                sp.wait_ge(x1_done, b + 1)
                sp.dma_start(h_t[:], h_scr[bass.ds(b, 1)].rearrange("o (t p) d -> p (o t) d", p=P)).then_inc(h_loaded, 16)
                sp.wait_ge(x1_done, b + 2)
                sp.dma_start(x1_scr[bass.ds(b, 1)].rearrange("o (t p) d -> p (o t) d", p=P), x1[:]).then_inc(x1_stored, 16)
                sp.wait_ge(rinv_done, b + 1)
                sp.dma_start(rinv_scr[bass.ds(b, 1)].rearrange("o p t -> (o p) t"), row_inv[:]).then_inc(rinv_stored, 16)
                sp.wait_ge(tr_dve, (b + 2) * ST)
                sp.dma_start(pT_scr[bass.ds(b, 1)].rearrange("o p t l -> (o p) t l"), pT[:]).then_inc(pT_stored, 16)
                sp.wait_ge(sT_done, (b + 2) * (KM * SH))
                for k in range(KM):
                    dst = sT_scr[:, k].rearrange("e p (b s) -> b p e s", s=SE)[bass.ds(b, 1)]
                    sp.dma_start(dst.rearrange("o p e s -> (o p) e s"),
                                 sT[:, k].rearrange("p (e s) -> p e s", s=SE)).then_inc(sT_stored, 16)
            for s, n in stores:
                sp.wait_ge(s, (B + 1) * n * 16)

        @block.scalar
        def _(act):
            for k in range(KM):
                for s in range(SH):
                    i = k * SH + s
                    act.wait_ge(seT_ps, i + 1)
                    act.activation(seT[:, k, s * HALF:(s + 1) * HALF], trans[:, i % 2], ACT.Copy).then_inc(seT_done, 1)
            for s, n in ((tr_act, ST), (exp_done, ST), (sT_done, KM * SH)):
                act.sem_inc(s, n)
            with act.Fori(0, B, 1) as b:
                tr0 = act.snap(b * TRS)
                for k in range(KM):
                    act.wait_ge(tr_done, tr0 + (USE_X + k + 1))
                    act.activation(xnT[:, k], trans[:, k], ACT.Copy).then_inc(xnT_done, 1)

                def combine_rows(t):
                    act.wait_ge(rmax_done, b * LT + (t + 1))
                    act.activation(prob[:, t], rows_ps[:, t % 2], ACT.Exp, bias=row_max[:, t:t + 1],
                                   accum_out=row_sum[:, t:t + 1]).then_inc(prob_done, 1)

                def dispatch_cols(s):
                    act.wait_ge(cmax_done, b * ST + (s + 1))
                    act.activation(disp[:, s % 4], cols_ps[:, s % 2], ACT.Exp, bias=col_max[:, s:s + 1],
                                   accum_out=col_sum[:, s:s + 1]).then_inc(exp_done, 1)

                combine_rows(0)
                combine_rows(1)
                dispatch_cols(0)
                dispatch_cols(1)
                combine_rows(2)
                combine_rows(3)
                for s in range(ST):
                    act.wait_ge(tr_done, tr0 + (USE_E + 2 * s + 1))
                    act.activation(dispT[:, :, s * P:(s + 1) * P], trans[:, s * 2 % 2].rearrange("p (t n) -> p t n", t=LT),
                                   ACT.Copy).then_inc(tr_act, 1)
                    if s + 2 < ST:
                        dispatch_cols(s + 2)
                act.wait_ge(sT_stored, (b + 1) * (KM * 16))
                for i in range(KM * SH):
                    act.wait_ge(slot_done, b * (KM * SH) + (i + 1 + KM * SH))
                    act.activation(sT[:, i // SH, (i % SH) * HALF:(i % SH + 1) * HALF],
                                   rows_ps[:, i // SH, (i % SH) * HALF:(i % SH + 1) * HALF], ACT.Copy).then_inc(sT_done, 1)

        @block.vector
        def _(dve):
            count = [0]
            base = [None]

            def link(ins):
                count[0] += 1
                ins.then_inc(chain, 1)
                dve.wait_ge(chain, count[0] if base[0] is None else base[0] + count[0])

            dve.wait_ge(c_loaded, 6 * 16)
            norm_steps(dve, link, se, se, se_stats, se_mv, se_rstd, se_tmp, se_normed)
            dve.wait_ge(se_normed, 1)
            for t in range(ST):
                ins = dve.tensor_tensor(se[:, t], se[:, t], sg_bc[:], ALU.mult)
            link(ins)
            for t in range(ST):
                ins = dve.tensor_tensor(se[:, t], se[:, t], sb_bc[:], ALU.add)
            link(ins)
            dve.tensor_scalar(se[:], se[:], scale_bc[:, 0:1], None, ALU.mult).then_inc(se_done, 1)
            before, count[0] = count[0], 0
            dve.sem_inc(x1_done, 1)
            dve.sem_inc(tr_dve, ST)
            PER = 2 * NORM_LINKS + 1
            with dve.Fori(0, B, 1) as b:
                base[0] = dve.snap(b * PER + before)
                tr0 = dve.snap(b * TRS)
                dve.wait_ge(h_loaded, (b + 1) * 16)
                dve.wait_ge(x1_stored, (b + 1) * 16)
                norm_steps(dve, link, h_t, x1, stats, mv, rstd, tmp, x1_done)
                dve.wait_ge(x1_done, b + 2)
                dve.wait_ge(slot_done, (b + 1) * (KM * SH))
                norm_steps(dve, link, x1, xn, stats, mv, rstd, tmp, xn_normed)
                dve.wait_ge(xn_normed, b + 1)
                for t in range(LT):
                    ins = dve.tensor_tensor(xn[:, t], xn[:, t], g_bc[:], ALU.mult)
                link(ins)
                for t in range(LT):
                    ins = dve.tensor_tensor(xn[:, t], xn[:, t], b_bc[:], ALU.add)
                ins.then_inc(xn_done, 1)
                assert count[0] == PER, count[0]

                def row_maximum(t):
                    dve.wait_ge(rows_done, b * LT + (t + 1))
                    dve.tensor_reduce(row_max[:, t:t + 1], rows_ps[:, t % 2], AX_X, ALU.max, negate=True).then_inc(rmax_done, 1)

                def col_maximum(s):
                    dve.wait_ge(cols_done, b * ST + (s + 1))
                    dve.tensor_reduce(col_max[:, s:s + 1], cols_ps[:, s % 2], AX_X, ALU.max, negate=True).then_inc(cmax_done, 1)

                def normalise(s):
                    dve.wait_ge(exp_done, b * ST + (s + 1 + ST))
                    dve.reciprocal(col_inv[:, s:s + 1], col_sum[:, s:s + 1]).then_inc(cinv_done, 1)
                    dve.wait_ge(cinv_done, b * ST + (s + 1))
                    dve.tensor_scalar(disp[:, s % 4], disp[:, s % 4], col_inv[:, s:s + 1], None, ALU.mult).then_inc(disp_done, 1)

                row_maximum(0)
                row_maximum(1)
                col_maximum(0)
                col_maximum(1)
                row_maximum(2)
                row_maximum(3)
                normalise(0)
                normalise(1)
                dve.wait_ge(prob_done, (b + 1) * LT)
                dve.wait_ge(rinv_stored, (b + 1) * 16)
                dve.reciprocal(row_inv[:], row_sum[:]).then_inc(rinv_done, 1)
                dve.wait_ge(pT_stored, (b + 1) * 16)
                for s in range(ST):
                    if s + 2 < ST:
                        col_maximum(s + 2)
                    dve.wait_ge(tr_done, tr0 + (USE_P + 2 * s + 1))
                    dve.tensor_copy(pT[:, s], trans[:, 1]).then_inc(tr_dve, 1)
                    if s + 2 < ST:
                        normalise(s + 2)

        @block.tensor
        def _(pe):
            pe.wait_ge(ident_done, 2)
            pe.wait_ge(se_done, 1)
            for k in range(KM):
                for s in range(SH):
                    i = k * SH + s
                    if i >= 2:
                        pe.wait_ge(seT_done, i - 1)
                    for t in range(HALF // P):
                        mm = pe.transpose(trans[:, i % 2, t * P:(t + 1) * P],
                                          se[:, s * (HALF // P) + t, k * P:(k + 1) * P], ident[:])
                    mm.then_inc(seT_ps, 1)
            pe.wait_ge(seT_done, KM * SH)
            pe.sem_inc(slot_done, KM * SH)
            with pe.Fori(0, B, 1) as b:
                pe.wait_ge(xn_done, b + 1)
                pe.wait_ge(tr_act, (b + 1) * ST)
                pe.wait_ge(tr_dve, (b + 1) * ST)
                for k in range(KM):
                    for t in range(LT):
                        mm = pe.transpose(trans[:, k, t * P:(t + 1) * P], xn[:, t, k * P:(k + 1) * P], ident[:])
                    mm.then_inc(tr_done, 1)
                pe.wait_ge(xnT_done, (b + 1) * KM)

                def rows(t):
                    if t < 2:
                        pe.wait_ge(sT_done, (b + 1) * (KM * SH))
                    else:
                        pe.wait_ge(prob_done, b * LT + (t - 1))
                    for s in range(SH):
                        for k in range(KM):
                            mm = pe.matmul(rows_ps[:, t % 2, s * HALF:(s + 1) * HALF], xnT[:, k, t * P:(t + 1) * P],
                                           seT[:, k, s * HALF:(s + 1) * HALF], start=(k == 0), stop=(k == KM - 1))
                    mm.then_inc(rows_done, 1)

                def cols(s):
                    if s < 2:
                        pe.wait_ge(exp_done, (b + 1) * ST)
                    else:
                        pe.wait_ge(exp_done, b * ST + (s - 1 + ST))
                    for k in range(KM):
                        mm = pe.matmul(cols_ps[:, s % 2], seT[:, k, s * P:(s + 1) * P], xnT[:, k],
                                       start=(k == 0), stop=(k == KM - 1))
                    mm.then_inc(cols_done, 1)

                rows(0)
                rows(1)
                cols(0)
                cols(1)
                rows(2)
                rows(3)
                for s in range(ST):
                    pe.wait_ge(disp_done, b * ST + (s + 1))
                    if s >= 1:
                        pe.wait_ge(tr_act, b * ST + (s + ST))
                    for t in range(LT):
                        mm = pe.transpose(trans[:, 0, t * P:(t + 1) * P], disp[:, s % 4, t * P:(t + 1) * P], ident[:])
                    mm.then_inc(tr_done, 1)
                    if s + 2 < ST:
                        cols(s + 2)
                    if s == 0:
                        pe.wait_ge(prob_done, (b + 1) * LT)
                    else:
                        pe.wait_ge(tr_dve, b * ST + (s + ST))
                    for t in range(LT):
                        mm = pe.transpose(trans[:, 1, t * P:(t + 1) * P], prob[:, t, s * P:(s + 1) * P], ident[:])
                    mm.then_inc(tr_done, 1)
                pe.wait_ge(tr_act, (b + 2) * ST)
                for k in range(KM):
                    for s in range(SH):
                        for t in range(LT):
                            mm = pe.matmul(rows_ps[:, k, s * HALF:(s + 1) * HALF], xn[:, t, k * P:(k + 1) * P],
                                           dispT[:, t, s * HALF:(s + 1) * HALF], start=(t == 0), stop=(t == LT - 1))
                        mm.then_inc(slot_done, 1)


def expert_stage(nc, sT_scr, Wg, bg, Wu, bu, Wd, bd, eo_scr):
    E, KM, _, ROWS = sT_scr.shape
    F, DO = Wd.shape[1:]
    B = eo_scr.shape[0]
    SE = ROWS // B
    KF = F // P
    NT = min(512, ROWS)
    HALVES, RT = ROWS // NT, ROWS // P
    UNITS = HALVES * KF
    NB = P // SE

    with ExitStack() as ctx:
        def sb(name, shape):
            return ctx.enter_context(nc.sbuf_tensor(name, shape, F32))

        def sem(name):
            return ctx.enter_context(nc.semaphore("x_" + name))

        gate_ps = ctx.enter_context(nc.psum_tensor("x_gate", [P, 2, 512], F32))
        up_ps = ctx.enter_context(nc.psum_tensor("x_up", [P, 2, 512], F32))
        down_ps = ctx.enter_context(nc.psum_tensor("x_down", [P, 4, 512], F32))
        wg = [sb(f"x_wg{q}", [P, KM, F]) for q in range(2)]
        wu = [sb(f"x_wu{q}", [P, KM, F]) for q in range(2)]
        wd = [sb(f"x_wd{q}", [P, KF, DO]) for q in range(2)]
        bd_bc = [sb(f"x_bd{q}", [P, DO]) for q in range(2)]
        xT = [sb(f"x_xT{q}", [P, KM, ROWS]) for q in range(2)]
        bg_t = [sb(f"x_bg{q}", [P, KF]) for q in range(2)]
        bu_t = [sb(f"x_bu{q}", [P, KF]) for q in range(2)]
        act_t = sb("x_act", [P, 4, NT])
        hT = [sb(f"x_hT{q}", [P, KF, ROWS]) for q in range(2)]
        eo = [sb(f"x_eo{q}", [P, RT, DO]) for q in range(2)]

        in_loaded = [sem(f"in_loaded{q}") for q in range(2)]
        gate_done, up_done, act_done, h_done = sem("gate_done"), sem("up_done"), sem("act_done"), sem("h_done")
        down_done, eo_done = sem("down_done"), sem("eo_done")
        eo_stored = [sem(f"eo_stored{q}") for q in range(2)]
        LOADS = 7

        block = ctx.enter_context(nc.Block())

        @block.sync
        def _(sp):

            def load(e, q):
                one = bass.ds(e, 1)
                sp.wait_ge(eo_done, e * RT)
                sp.dma_start(xT[q][:], sT_scr[one].rearrange("o k p r -> p (o k) r")).then_inc(in_loaded[q], 16)
                sp.dma_start(wg[q][:], Wg[one].rearrange("o (k p) f -> p (o k) f", p=P)).then_inc(in_loaded[q], 16)
                sp.dma_start(wu[q][:], Wu[one].rearrange("o (k p) f -> p (o k) f", p=P)).then_inc(in_loaded[q], 16)
                sp.dma_start(wd[q][:], Wd[one].rearrange("o (k p) f -> p (o k) f", p=P)).then_inc(in_loaded[q], 16)
                sp.dma_start(bd_bc[q][:], bd[one].broadcast_to([P, DO])).then_inc(in_loaded[q], 16)
                sp.dma_start(bg_t[q][:], bg[one].rearrange("o p k -> (o p) k")).then_inc(in_loaded[q], 16)
                sp.dma_start(bu_t[q][:], bu[one].rearrange("o p k -> (o p) k")).then_inc(in_loaded[q], 16)

            def store(e, q):
                sp.wait_ge(eo_done, (e + 2) * RT)
                for n in range(NB):
                    dst = eo_scr.rearrange("(t n) (e s) o -> e n s t o", n=NB, s=SE)[bass.ds(e, 1), n]
                    sp.dma_start(dst.rearrange("e s t o -> (e s) t o"),
                                 eo[q][n * SE:(n + 1) * SE]).then_inc(eo_stored[q], 16)

            for q in range(2):
                sp.sem_inc(eo_stored[q], NB * 16)
            load(0, 0)
            with sp.Fori(0, E - 2, 2) as e:
                load(e + 1, 1)
                store(e, 0)
                load(e + 2, 0)
                store(e + 1, 1)
            load(E - 1, 1)
            store(E - 2, 0)
            store(E - 1, 1)
            for q in range(2):
                sp.wait_ge(eo_stored[q], (E // 2 + 1) * NB * 16)

        @block.scalar
        def _(act):
            with act.Fori(0, E // 2, 1) as e2:
                for q in range(2):
                    for i in range(UNITS):
                        c, done = i % KF, q * UNITS + i + 1
                        act.wait_ge(gate_done, e2 * (2 * UNITS) + done)
                        act.wait_ge(h_done, e2 * (2 * UNITS) + done)
                        act.activation(act_t[:, i % 4], gate_ps[:, i % 2, 0:NT], ACT.Gelu,
                                       bias=bg_t[q][:, c:c + 1]).then_inc(act_done, 1)

        @block.vector
        def _(dve):
            dve.sem_inc(h_done, 4)
            dve.sem_inc(eo_done, RT)
            with dve.Fori(0, E // 2, 1) as e2:
                for q in range(2):
                    dve.wait_ge(in_loaded[q], (e2 + 1) * (LOADS * 16))
                    for i in range(UNITS):
                        c, r, done = i % KF, i // KF, q * UNITS + i + 1
                        dve.wait_ge(up_done, e2 * (2 * UNITS) + done)
                        dve.wait_ge(act_done, e2 * (2 * UNITS) + done)
                        dve.scalar_tensor_tensor(out=hT[q][:, c, r * NT:(r + 1) * NT], in0=up_ps[:, i % 2, 0:NT],
                                                 scalar=bu_t[q][:, c:c + 1],
                                                 in1=act_t[:, i % 4], op0=ALU.add, op1=ALU.mult).then_inc(h_done, 1)
                    dve.wait_ge(eo_stored[q], (e2 + 1) * (NB * 16))
                    for t in range(RT):
                        dve.wait_ge(down_done, e2 * (2 * RT) + (q * RT + t + 1))
                        dve.tensor_tensor(eo[q][:, t], down_ps[:, t % 4, 0:DO], bd_bc[q][:], ALU.add).then_inc(eo_done, 1)

        @block.tensor
        def _(pe):
            with pe.Fori(0, E // 2, 1) as e2:
                for q in range(2):
                    pe.wait_ge(in_loaded[q], (e2 + 1) * (LOADS * 16))
                    for i in range(UNITS):
                        c, r, done = i % KF, i // KF, q * UNITS + i + 1
                        pe.wait_ge(h_done, e2 * (2 * UNITS) + (done + 2))
                        for k in range(KM):
                            mm = pe.matmul(gate_ps[:, i % 2, 0:NT], wg[q][:, k, c * P:(c + 1) * P],
                                           xT[q][:, k, r * NT:(r + 1) * NT], start=(k == 0), stop=(k == KM - 1))
                        mm.then_inc(gate_done, 1)
                        for k in range(KM):
                            mm = pe.matmul(up_ps[:, i % 2, 0:NT], wu[q][:, k, c * P:(c + 1) * P],
                                           xT[q][:, k, r * NT:(r + 1) * NT], start=(k == 0), stop=(k == KM - 1))
                        mm.then_inc(up_done, 1)
                    for t in range(RT):
                        half = t * P // NT + 1
                        pe.wait_ge(h_done, e2 * (2 * UNITS) + (q * UNITS + half * KF + 4))
                        pe.wait_ge(eo_done, e2 * (2 * RT) + (q * RT + t - 3 + RT))
                        for c in range(KF):
                            mm = pe.matmul(down_ps[:, t % 4, 0:DO], hT[q][:, c, t * P:(t + 1) * P], wd[q][:, c],
                                           start=(c == 0), stop=(c == KF - 1))
                        mm.then_inc(down_done, 1)


def merge_stage(nc, pT_scr, rinv_scr, x1_scr, eo_scr, out):
    B, _, ST, L = pT_scr.shape
    DM = out.shape[-1]
    LT = L // P

    with ExitStack() as ctx:
        def sb(name, shape):
            return ctx.enter_context(nc.sbuf_tensor(name, shape, F32))

        def sem(name):
            return ctx.enter_context(nc.semaphore("m_" + name))

        acc = ctx.enter_context(nc.psum_tensor("m_acc", [P, 2, LT, 512], F32))
        pT = [sb(f"m_pT{q}", [P, ST, L]) for q in range(2)]
        eo = [sb(f"m_eo{q}", [P, ST, DM]) for q in range(2)]
        x1 = [sb(f"m_x1{q}", [P, LT, DM]) for q in range(2)]
        rinv = [sb(f"m_rinv{q}", [P, LT]) for q in range(2)]
        y = sb("m_y", [P, LT, DM])
        out_t = [sb(f"m_out{q}", [P, LT, DM]) for q in range(2)]
        stats, mv = sb("m_stats", [P, LT, 6]), sb("m_mv", [P, LT, 2])
        rstd, tmp = sb("m_rstd", [P, LT]), sb("m_tmp", [P, LT])

        in_loaded = [sem(f"in_loaded{q}") for q in range(2)]
        acc_done, y_done, chain, out_done = sem("acc_done"), sem("y_done"), sem("chain"), sem("out_done")
        stored = [sem(f"stored{q}") for q in range(2)]

        block = ctx.enter_context(nc.Block())

        @block.sync
        def _(sp):
            def load(b, q):
                one = bass.ds(b, 1)
                sp.wait_ge(out_done, b)
                sp.dma_start(pT[q][:], pT_scr[one].rearrange("o p t l -> (o p) t l")).then_inc(in_loaded[q], 16)
                sp.dma_start(eo[q][:], eo_scr[one].rearrange("o (t p) d -> p (o t) d", p=P)).then_inc(in_loaded[q], 16)
                sp.dma_start(x1[q][:], x1_scr[one].rearrange("o (t p) d -> p (o t) d", p=P)).then_inc(in_loaded[q], 16)
                sp.dma_start(rinv[q][:], rinv_scr[one].rearrange("o p t -> (o p) t")).then_inc(in_loaded[q], 16)

            def store(b, q):
                sp.wait_ge(out_done, b + 2)
                sp.dma_start(out[bass.ds(b, 1)].rearrange("o (t p) d -> p (o t) d", p=P), out_t[q][:]).then_inc(stored[q], 16)

            for q in range(2):
                sp.sem_inc(stored[q], 16)
            load(0, 0)
            if B > 2:
                with sp.Fori(0, B - 2, 2) as b:
                    load(b + 1, 1)
                    store(b, 0)
                    load(b + 2, 0)
                    store(b + 1, 1)
            load(B - 1, 1)
            store(B - 2, 0)
            store(B - 1, 1)
            for q in range(2):
                sp.wait_ge(stored[q], (B // 2 + 1) * 16)

        @block.vector
        def _(dve):
            PER = NORM_LINKS
            dve.sem_inc(out_done, 1)
            dve.sem_inc(y_done, 2 * LT)
            with dve.Fori(0, B // 2, 1) as b2:
                for q in range(2):
                    count = [q * PER]

                    def link(ins):
                        count[0] += 1
                        ins.then_inc(chain, 1)
                        dve.wait_ge(chain, b2 * (2 * PER) + count[0])

                    dve.wait_ge(out_done, b2 * 2 + (q + 1))
                    dve.wait_ge(in_loaded[q], (b2 + 1) * (4 * 16))
                    for t in range(LT):
                        i = q * LT + t + 1
                        dve.wait_ge(acc_done, b2 * (2 * LT) + i)
                        dve.scalar_tensor_tensor(out=y[:, t], in0=acc[:, q, t, 0:DM], scalar=rinv[q][:, t:t + 1],
                                                 in1=x1[q][:, t], op0=ALU.mult, op1=ALU.add).then_inc(y_done, 1)
                    dve.wait_ge(y_done, (b2 + 1) * (2 * LT) + (q + 1) * LT)
                    dve.wait_ge(stored[q], (b2 + 1) * 16)
                    norm_steps(dve, link, y, out_t[q], stats, mv, rstd, tmp, out_done)
                    assert count[0] == (q + 1) * PER

        @block.tensor
        def _(pe):
            with pe.Fori(0, B // 2, 1) as b2:
                for q in range(2):
                    pe.wait_ge(in_loaded[q], (b2 + 1) * (4 * 16))
                    pe.wait_ge(y_done, (b2 + 1) * (2 * LT))
                    for t in range(LT):
                        for s in range(ST):
                            mm = pe.matmul(acc[:, q, t, 0:DM], pT[q][:, s, t * P:(t + 1) * P], eo[q][:, s],
                                           start=(s == 0), stop=(s == ST - 1))
                        mm.then_inc(acc_done, 1)


def build(nc, a, out):
    x = a["x"]
    B, L, DM = x.shape
    N = a["A_log"].shape[-1]
    E, DM, F = a["Wg"].shape
    S = a["slots"].shape[0]
    h = nc.dram_tensor("h_scr", (B, L, DM), F32).ap()
    x1 = nc.dram_tensor("x1_scr", (B, L, DM), F32).ap()
    pT = nc.dram_tensor("pT_scr", (B, P, S // P, L), F32).ap()
    rinv = nc.dram_tensor("rinv_scr", (B, P, L // P), F32).ap()
    sT = nc.dram_tensor("sT_scr", (E, DM // P, P, B * (S // E)), F32).ap()
    eo = nc.dram_tensor("eo_scr", (B, S, DM), F32).ap()
    bc = nc.dram_tensor("bc_scr", (B, 2, 2 * N, L), F32).ap()
    mixer_stage(nc, a["x_T"], x, a["in_proj_T"], a["conv_w"], a["conv_b"], a["x_proj_T"], a["dt_proj_T"],
                a["dt_proj_b"], a["A_log"], a["D"], a["out_proj_T"], h, bc)
    route_stage(nc, h, a["slots"], a["slot_g"], a["slot_b"], a["scale"], a["norm_g"], a["norm_b"], x1, pT, rinv, sT)
    expert_stage(nc, sT, a["Wg"], a["bg"], a["Wu"], a["bu"], a["Wd"], a["bd"], eo)
    merge_stage(nc, pT, rinv, x1, eo, out)


def kernel(**inputs):
    import numpy as np
    import concourse.bacc as bacc
    from concourse.bass_utils import run_bass_kernel_spmd

    at = {k.split("_", 2)[2]: np.asarray(v) for k, v in inputs.items() if k.startswith("L0_attn_")}
    ff = {k.split("_", 2)[2]: np.asarray(v) for k, v in inputs.items() if k.startswith("L0_ffn_")}
    both = lambda f, g: np.stack([at[f], at[g]])

    def chunked(v):
        return np.moveaxis(v.reshape(v.shape[0], -1, P, *v.shape[2:]), 2, 0)

    data = {
        "x_T": at["x"].transpose(0, 2, 1),
        "x": at["x"],
        "in_proj_T": at["in_proj_w"].T,
        "conv_w": chunked(both("conv_w", "conv_b_w")[:, :, 0]),
        "conv_b": chunked(both("conv_b", "conv_b_b")),
        "x_proj_T": chunked(both("x_proj_w", "x_proj_b_w").transpose(0, 2, 1)),
        "dt_proj_T": both("dt_proj_w", "dt_proj_b_w").transpose(0, 2, 1),
        "dt_proj_b": chunked(both("dt_proj_b", "dt_proj_b_b")),
        "A_log": chunked(both("A_log", "A_b_log")),
        "D": chunked(both("D", "D_b")),
        "out_proj_T": at["out_proj_w"].T,
        "slots": ff["slot_embeds"].reshape(-1, ff["slot_embeds"].shape[-1]),
        "bg": chunked(ff["bg"]).swapaxes(0, 1),
        "bu": chunked(ff["bu"]).swapaxes(0, 1),
        **{n: ff[n] for n in ("slot_g", "slot_b", "scale", "norm_g", "norm_b", "Wg", "Wu", "Wd", "bd")},
    }
    nc = bacc.Bacc("TRN2", target_bir_lowering=False, num_devices=1)
    arrays, aps = {}, {}
    for name, v in data.items():
        arrays[f"in_{name}"] = np.ascontiguousarray(v)
        aps[name] = nc.dram_tensor(f"in_{name}", v.shape, mybir.dt.from_np(v.dtype), kind="ExternalInput").ap()
    out = nc.dram_tensor("out", at["x"].shape, F32, kind="ExternalOutput").ap()
    build(nc, aps, out)
    r = run_bass_kernel_spmd(nc, [arrays], core_ids=[0])
    return r.results[0]["out"]
```

```python
from contextlib import ExitStack
import math

import concourse.bass as bass
from concourse import mybir

F32 = mybir.dt.float32
I32 = mybir.dt.int32
ALU = mybir.AluOpType
ACT = mybir.ActivationFunctionType
AX_X = mybir.AxisListType.X
P = 128

LN_EPS = 1e-5
SCAN_EPS = 1e-12
HALF_NEG_LN_EPS = -0.5 * math.log(SCAN_EPS)


def halves(t):
    return t.rearrange("p a b -> p (a b)")


def make_identity(eng, ident, done):
    eng.memset(ident[:], 0.0).then_inc(done, 1)
    eng.wait_ge(done, 1)
    eng.affine_select(out=ident[:], in_=ident[:], compare_op=ALU.not_equal, fill=1.0, base=0,
                      pattern=[[-1, P]], channel_multiplier=1).then_inc(done, 1)


NORM_STEPS = 2 + 3 + 3 * 3 + 1


def norm_step(dve, k, link, src, dst, stats, mv, rstd, tmp, done):
    rows = src.shape[1]
    var = mv[:, :, 1]
    if k == 0:
        for t in range(rows):
            ins = dve.bn_stats(stats[:, t], src[:, t])
        link(ins)
    elif k == 1:
        dve.memset(tmp[:], 0.0)
        for t in range(rows):
            ins = dve.bn_aggr(mv[:, t], stats[:, t])
        link(ins)
    elif k == 2:
        link(dve.tensor_scalar(var, var, LN_EPS, None, ALU.add))
    elif k == 3:
        link(dve.tensor_scalar(tmp[:].bitcast(I32), var.bitcast(I32), 1, None, ALU.arith_shift_right))
    elif k == 4:
        link(dve.tensor_scalar(rstd[:].bitcast(I32), tmp[:].bitcast(I32), -1.0, float(0x5F3759DF), ALU.mult, ALU.add))
    elif k < NORM_STEPS - 1:
        if (k - 5) % 3 == 0:
            link(dve.scalar_tensor_tensor(out=tmp[:], in0=rstd[:], scalar=-0.5, in1=rstd[:], op0=ALU.mult, op1=ALU.mult))
        elif (k - 5) % 3 == 1:
            link(dve.tensor_tensor(tmp[:], tmp[:], var, ALU.mult))
        else:
            link(dve.scalar_tensor_tensor(out=rstd[:], in0=tmp[:], scalar=1.5, in1=rstd[:], op0=ALU.add, op1=ALU.mult))
    else:
        for t in range(rows):
            ins = dve.tensor_scalar(dst[:, t], src[:, t], mv[:, t, 0:1], rstd[:, t:t + 1], ALU.subtract, ALU.mult)
        ins.then_inc(done, 1)


NORM_LINKS = NORM_STEPS - 1


def norm_steps(dve, link, src, dst, stats, mv, rstd, tmp, done):
    for k in range(NORM_STEPS):
        norm_step(dve, k, link, src, dst, stats, mv, rstd, tmp, done)


def timetable():
    order = """
        res0 conv1_0 out0 out1 out2 out3 conv1_1 res1 conv1_2 res2 conv1_3 res3 x1_0 dt1_0 dt1_1 xnT0 xnT1
        rows0 rows1 dt1_2 cols0 cols1 rowsT0 rowsT1 dt1_3 colsT0 colsT1 slots0 slots1
        rows2 rows3 cols2 cols3 rowsT2 rowsT3 colsT2 in0_0 colsT3 in0_1 slots2 in0_2 slots3 in0_3 conv0_0
        rows4 conv0_1 rows5 conv0_2 cols4 cols5 conv0_3 rowsT4 rowsT5 x0_0 colsT4 colsT5 slots4 slots5 dt0_0
        rows6 rows7 dt0_1 cols6 cols7 dt0_2 dt0_3 rowsT6 rowsT7 colsT6 colsT7 slots6 slots7"""
    return [(name[:-1].rstrip("_"), int(name[-1])) for name in order.split()]


WEIGHT = {"out": 2.0, "res": 3.4, "conv0": 5.2, "conv1": 5.2, "x0": 4.4, "x1": 4.4, "dt0": 5.0, "dt1": 5.0, "in0": 2.2,
          "xnT": 0.8, "rows": 3.3, "cols": 3.4, "rowsT": 1.0, "colsT": 1.0, "slots": 2.2}
IN_TILE = 64


def slot_tiles(table, last, seg):
    tiles, first_in = [], table.index(("in0", 0))
    for slots, begin, end in ((table[:first_in], 0, IN_TILE), (table[first_in:], IN_TILE, last)):
        turns = [t for t in range(begin, end) if t % seg >= 3]
        total, before = sum(WEIGHT[kind] for kind, _ in slots), 0.0
        for kind, _ in slots:
            tile = turns[int(before / total * len(turns))]
            tiles.append(max([tile] + tiles[-1:] + [t + 2 for t in tiles[-2:-1]]))
            before += WEIGHT[kind]
    return tiles


PROLOGUE = ("in0", "conv0", "x0", "dt0")
EPILOGUE = ("out", "xnT", "rows", "cols", "rowsT", "colsT", "slots")


def sequence_stage(nc, xT, x, in_wT, conv_w, conv_b, x_wT, dt_wT, dt_b, A_log, D, out_wT,
                   slot_e, slot_g, slot_b, scale, norm_g, norm_b, bc_scr, x1_scr, pT_scr, rinv_scr, sT_scr):
    B, L, DM = x.shape
    DI = in_wT.shape[1] // 2
    NDIR, R, _ = dt_wT.shape
    N = A_log.shape[-1]
    KC = conv_w.shape[-1]
    KM, KI, LT = DM // P, DI // P, L // P
    S = slot_e.shape[0]
    E = sT_scr.shape[0]
    SE = S // E
    ST = S // P
    HS = 512
    PAD = KC - 1
    PAIRS = KI // 2
    SEG = 2 * N
    TILES = NDIR * PAIRS * SEG
    assert L == 512 and KI == 4 and KM == 2 and LT == 4 and S == 2 * HS and N == 16

    TABLE = timetable()
    SLOTS = len(TABLE)
    PRO = [s for s, (k, _) in enumerate(TABLE) if k in PROLOGUE]
    EPI = [s for s, (k, _) in enumerate(TABLE) if k in EPILOGUE]
    tile_of = slot_tiles(TABLE, TILES - 6, SEG)
    SKIPS = {10: ((0, 0, 0),), 14: ((0, 1, 0),), 26: ((1, 0, 0),), 29: ((1, 1, 0),),
             38: ((0, 0, 1),), 42: ((0, 1, 1),), 50: ((1, 0, 1),), 54: ((1, 1, 1),)}
    NORM_TILE = 14
    CR = 256

    VR = 6
    RING = [i % 3 for i in range(TILES // 2)]
    RING[-1] = 1

    def slots_at(t, kinds):
        return [s for s in range(SLOTS) if tile_of[s] == t and TABLE[s][0] in kinds]

    def chunk_of(t):
        return (t // SEG) % PAIRS * 2 + t % 2

    def dir_of(t):
        return t // (PAIRS * SEG)

    def state_of(t):
        return t % SEG // 2

    with ExitStack() as ctx:
        def sb(name, shape):
            return ctx.enter_context(nc.sbuf_tensor(name, shape, F32))

        def sem(name):
            return ctx.enter_context(nc.semaphore(name))

        y_ps = ctx.enter_context(nc.psum_tensor("y_ps", [P, 2, 512], F32))
        e_ps = ctx.enter_context(nc.psum_tensor("e_ps", [P, 2, 512], F32))
        f_ps = ctx.enter_context(nc.psum_tensor("f_ps", [P, 2, 512], F32))
        side = ctx.enter_context(nc.psum_tensor("side", [P, 2, 512], F32))

        w_in = sb("w_in", [P, KM, 2 * DI])
        w_conv = sb("w_conv", [P, NDIR, KI, KC])
        b_conv_half = sb("b_conv_half", [P, NDIR, KI])
        w_x = sb("w_x", [P, NDIR, KI, R + 2 * N])
        w_dt = sb("w_dt", [R, NDIR, DI])
        b_dt = sb("b_dt", [P, NDIR, KI])
        d_skip = sb("d_skip", [P, NDIR, KI])
        w_out = sb("w_out", [P, KI, DM])
        a_neg = sb("a_neg", [P, NDIR, KI, N])
        a_neg_half = sb("a_neg_half", [P, NDIR, KI, N])
        guard_bias = sb("guard_bias", [P, 1])
        one = sb("one", [P, 1])
        ident = sb("ident", [P, P])
        conv_diag = sb("conv_diag", [P, NDIR, KI, KC, P])
        d_diag = sb("d_diag", [P, NDIR, KI, P])
        seT = sb("seT", [P, KM, S])
        g_col, b_col = sb("g_col", [P, KM]), sb("b_col", [P, KM])

        xT_t = sb("xT_t", [P, KM, L])
        u = [sb(f"u{d}", [P, KI, PAD + L]) for d in range(NDIR)]
        xf_pad = u[1]
        res_gate = sb("res_gate", [P, KI, L])
        xdbl = sb("xdbl", [R + 2 * N, L])
        dt = [sb(f"dt{d}", [P, KI, L]) for d in range(NDIR)]
        dtu = [sb(f"dtu{d}", [P, KI, L]) for d in range(NDIR)]
        rsum = [sb(f"rsum{d}", [P, KI, L]) for d in range(NDIR)]
        sp_exp, sp_one = dtu, rsum
        conv_tanh, res_tanh = dt, dtu[1]
        yg = sb("yg", [P, KI, L])
        x1 = sb("x1", [P, LT, DM])
        xn = sb("xn", [P, LT, DM])
        xnT = sb("xnT", [P, KM, L])
        stats, mv = sb("stats", [P, LT, 6]), sb("mv", [P, LT, 2])
        rstd, tmp = sb("rstd", [P, LT]), sb("tmp", [P, LT])
        se = dt[0][:].rearrange("p a (b c) -> p (a b) c", c=DM)
        sg_bc, sb_bc = xn[:, 0], xn[:, 1]
        row_max, row_sum, row_inv = sb("row_max", [P, LT]), sb("row_sum", [P, LT]), sb("row_inv", [P, LT])
        col_max, col_sum, col_inv = sb("col_max", [P, ST]), sb("col_sum", [P, ST]), sb("col_inv", [P, ST])

        b_ring, c_ring = sb("b_ring", [P, 3, L]), sb("c_ring", [P, 3, L])
        g_ring = sb("g_ring", [P, 4, L])
        s_ring = sb("s_ring", [P, 3, L])
        z_ring = sb("z_ring", [P, 3, L])
        v_ring = sb("v_ring", [P, VR, L])
        row_t = sb("row_t", [P, S])
        se_stats = row_t[:, 0:6 * ST].rearrange("p (a b) -> p a b", b=6)
        se_mv = row_t[:, 6 * ST:8 * ST].rearrange("p (a b) -> p a b", b=2)
        se_rstd, se_tmp = row_t[:, 8 * ST:9 * ST], row_t[:, 9 * ST:10 * ST]
        scale_bc = row_t[:, 10 * ST:10 * ST + 1]
        rowT_ring = sb("rowT_ring", [P, 2, L])
        disp_ring = sb("disp_ring", [P, 2, L])
        dispT_ring = sb("dispT_ring", [P, 2, L])
        sT_ring = sb("sT_ring", [P, 2, KM, P])

        w_loaded, ident_done, init_done, const_done, a_exp_done = (
            sem(n) for n in ("w_loaded", "ident_done", "init_done", "const_done", "a_exp_done"))
        sp_steps = sem("sp_steps")
        se_normed, se_done, seT_ps, seT_done = sem("se_normed"), sem("se_done"), sem("seT_ps"), sem("seT_done")
        xT_loaded, x_loaded, bc_stored = sem("xT_loaded"), sem("x_loaded"), sem("bc_stored")
        side_done = sem("side_done")
        side_free = [sem(f"side_free{q}") for q in range(2)]
        u0_done, u1_done, gate_done = sem("u0_done"), sem("u1_done"), sem("gate_done")
        exp_done, one_done, fix_done, ln_done = sem("exp_done"), sem("one_done"), sem("fix_done"), sem("ln_done")
        max_done, dt_done, rsum_done, dtu_done = sem("max_done"), sem("dt_done"), sem("rsum_done"), sem("dtu_done")
        f_ready, g_done, scan_done, z_done = sem("f_ready"), sem("g_done"), sem("scan_done"), sem("z_done")
        v_even, v_odd, v_used = sem("v_even"), sem("v_odd"), sem("v_used")
        y_evac, yg_done = sem("y_evac"), sem("yg_done")
        chain, x1_done, xn_normed = (
            sem(n) for n in ("chain", "x1_done", "xn_normed"))
        rmax_done, prob_done, rinv_done = sem("rmax_done"), sem("prob_done"), sem("rinv_done")
        cmax_done, cinv_done, disp_done = sem("cmax_done"), sem("cinv_done"), sem("disp_done")
        x1_stored, rinv_stored = sem("x1_stored"), sem("rinv_stored")
        u_done = (u0_done, u1_done)
        b_loaded = [sem(f"b_loaded{k}") for k in range(3)]
        c_loaded = [sem(f"c_loaded{k}") for k in range(3)]
        rowT_stored = [sem(f"rowT_stored{k}") for k in range(2)]
        sT_stored = [sem(f"sT_stored{k}") for k in range(2)]
        NW = 15

        class At:
            def __init__(self, mode, b, eng):
                self.mode, self.b = mode, b
                if mode == "loop":
                    self.slot0 = eng.snap(b * SLOTS + len(PRO))
                    self.half0 = eng.snap(b * (SLOTS // 2))
                    self.ahead = eng.snap(b + 1)

            def done(self, s):
                if self.mode == "loop":
                    return self.slot0 + (s + 1)
                return PRO.index(s) + 1 if self.mode == "pro" else len(PRO) + B * SLOTS + EPI.index(s) + 1

            def bank(self, s):
                return (len(PRO) + s) % 2 if self.mode == "loop" else (self.done(s) - 1) % 2

            def freed(self, s, more=1):
                if self.mode == "loop":
                    return self.half0 + ((len(PRO) + s) // 2 + more + CR)
                return (self.done(s) - 1) // 2 + more + CR

            def seq(self, d):
                if self.mode == "loop":
                    return self.ahead if d == 0 else self.b
                return 0 if self.mode == "pro" else B

        block = ctx.enter_context(nc.Block())

        @block.sync
        def _(sp):
            sp.dma_start(w_in[:], in_wT.rearrange("(k p) n -> p k n", p=P)).then_inc(w_loaded, 16)
            sp.dma_start(w_out[:], out_wT.rearrange("(k p) n -> p k n", p=P)).then_inc(w_loaded, 16)
            sp.dma_start(w_dt[:], dt_wT.rearrange("d r n -> r d n")).then_inc(w_loaded, 16)
            for dst, src in ((w_conv, conv_w), (b_conv_half, conv_b), (w_x, x_wT), (b_dt, dt_b), (d_skip, D), (a_neg, A_log)):
                sp.dma_start(dst[:], src).then_inc(w_loaded, 16)
            for dst, src in ((sg_bc, slot_g), (sb_bc, slot_b), (scale_bc, scale)):
                sp.dma_start(dst, src.rearrange("(o n) -> o n", o=1).broadcast_to([P, src.shape[0]])).then_inc(w_loaded, 16)
            for dst, src in ((g_col, norm_g), (b_col, norm_b)):
                sp.dma_start(dst[:], src).then_inc(w_loaded, 16)
            sp.dma_start(se, slot_e.rearrange("(t p) d -> p t d", p=P)).then_inc(w_loaded, 16)
            sp.dma_start(xT_t[:], xT[0].rearrange("(k p) l -> p k l", p=P)).then_inc(xT_loaded, 16)
            sp.dma_start(x1[:], x[0].rearrange("(t p) d -> p t d", p=P)).then_inc(x_loaded, 16)

            def go():
                sp.sem_inc(sp_steps, 1)

            def store_bc(at, d):
                s = TABLE.index(("x0", 0) if d == 0 else ("x1", 0))
                row = bass.ds(at.seq(d), 1) if at.mode == "loop" else slice(0, 1)
                sp.wait_ge(side_free[at.bank(s)], at.freed(s))
                go()
                sp.dma_start(bc_scr[row, d].rearrange("o m l -> (o m) l"), xdbl[R:R + 2 * N]).then_inc(bc_stored, 16)

            def load(at, i, c):
                d, n = i // (PAIRS * N), i % N
                ring, loaded = ((b_ring, b_loaded), (c_ring, c_loaded))[c]
                last = max(j for j in range(i - TILES // 2, i) if RING[j % (TILES // 2)] == RING[i])
                if c == 0:
                    sp.wait_ge(g_done, at.b * TILES + (2 * last + 2 + CR))
                else:
                    sp.wait_ge(v_even, at.b * (TILES // 2) + (last + 1 + CR))
                    sp.wait_ge(v_odd, at.b * (TILES // 2) + (last + 1 + CR))
                if i % (PAIRS * N) == 0 and c == 0:
                    sp.wait_ge(bc_stored, (at.b * 2 + (d + 1)) * 16)
                go()
                src = bc_scr[bass.ds(at.b, 1), d].rearrange("o m l -> (o m) l")[c * N + n:c * N + n + 1]
                sp.dma_start(ring[:, RING[i]], src.broadcast_to([P, L])).then_inc(loaded[RING[i]], 16)

            def store_rowT(at, i):
                row = bass.ds(at.seq(1), 1)
                s = TABLE.index(("rowsT", i))
                sp.wait_ge(side_free[at.bank(s)], at.freed(s))
                t, half = i // 2, i % 2
                dst = pT_scr[row, :, half * 4:half * 4 + 4, t * P:(t + 1) * P].rearrange("o p c l -> (o p) c l")
                go()
                sp.dma_start(dst, rowT_ring[:, i % 2].rearrange("p (c l) -> p c l", c=4)).then_inc(rowT_stored[i % 2], 16)

            def store_sT(at, i):
                s = TABLE.index(("slots", i))
                sp.wait_ge(side_free[at.bank(s)], at.freed(s))
                go()
                for k in range(KM):
                    dst = sT_scr[i * (P // SE):(i + 1) * (P // SE), k].rearrange("e p (b s) -> b p e s", s=SE)
                    dst = dst[bass.ds(at.seq(1), 1)].rearrange("o p e s -> (o p) e s")
                    sp.dma_start(dst, sT_ring[:, i % 2, k].rearrange("p (e s) -> p e s", s=SE)).then_inc(sT_stored[i % 2], 16)

            def store_x1(at):
                sp.wait_ge(x1_done, at.seq(1) + (1 + CR))
                go()
                sp.dma_start(x1_scr[bass.ds(at.seq(1), 1)].rearrange("o (t p) d -> p (o t) d", p=P), x1[:]).then_inc(x1_stored, 16)

            def store_rinv(at):
                sp.wait_ge(rinv_done, at.seq(1) + (1 + CR))
                go()
                sp.dma_start(rinv_scr[bass.ds(at.seq(1), 1)].rearrange("o p t -> (o p) t"), row_inv[:]).then_inc(rinv_stored, 16)

            sp.sem_inc(x1_stored, 16)
            sp.sem_inc(rinv_stored, 16)
            for q in range(2):
                sp.sem_inc(rowT_stored[q], 16)
                sp.sem_inc(sT_stored[q], KM * 16)
            store_bc(At("pro", None, sp), 0)

            def side_stores(at, t):
                for s in slots_at(t, ("x0", "x1", "rowsT", "slots", "xnT")):
                    kind, i = TABLE[s]
                    if kind == "x0":
                        store_bc(at, 0)
                    if kind == "x1":
                        store_bc(at, 1)
                    if kind == "xnT" and i == 0:
                        store_x1(at)
                    if kind == "rowsT":
                        store_rowT(at, i)
                    if kind == "slots":
                        store_sT(at, i)

            def steps(at, load_next_x):
                load(at, 0, 0)
                for i in range(TILES // 2):
                    if i + 1 < TILES // 2:
                        load(at, i + 1, 0)
                    load(at, i, 1)
                    if i >= 5:
                        for t in (2 * (i - 5), 2 * (i - 5) + 1):
                            side_stores(at, t)
                    if i == 24:
                        sp.wait_ge(xn_normed, at.b + (1 + CR))
                        sp.wait_ge(x1_stored, (at.b + 2) * 16)
                        go()
                        sp.dma_start(x1[:], x[bass.ds(at.b, 1)].rearrange("o (t p) d -> p (o t) d", p=P)).then_inc(x_loaded, 16)
                    if i == 28:
                        sp.wait_ge(gate_done, (at.b + 1) * KI)
                        go()
                        load_next_x()
                for t in range(TILES - 10, TILES):
                    side_stores(at, t)
                store_rinv(at)

            with sp.Fori(0, B - 1, 1) as b:
                steps(At("loop", b, sp), lambda: sp.dma_start(
                    xT_t[:], xT[bass.ds(b + 1, 1)].rearrange("o (k p) l -> p (o k) l", p=P)).then_inc(xT_loaded, 16))
            with sp.Fori(B - 1, B, 1) as b:
                steps(At("loop", b, sp), lambda: sp.dma_start(
                    xT_t[:], xT[0].rearrange("(k p) l -> p k l", p=P)).then_inc(xT_loaded, 16))
            with sp.Fori(B, B + 1, 1) as b:
                at = At("epi", b, sp)
                at.seq = lambda d: b
                for s in EPI:
                    kind, i = TABLE[s]
                    if kind == "xnT" and i == 0:
                        store_x1(at)
                    if kind == "rowsT":
                        store_rowT(at, i)
                    if kind == "slots":
                        store_sT(at, i)
                store_rinv(at)
            sp.wait_ge(x1_stored, (B + 2) * 16)
            sp.wait_ge(rinv_stored, (B + 2) * 16)
            sp.wait_ge(bc_stored, (2 * B + 1) * 16)
            for q in range(2):
                sp.wait_ge(rowT_stored[q], ((B + 1) * 4 + 1) * 16)
                sp.wait_ge(sT_stored[q], ((B + 1) * 4 + 1) * KM * 16)

        @block.gpsimd
        def _(pool):
            make_identity(pool, ident, ident_done)
            pool.sem_inc(v_odd, CR)
            pool.sem_inc(g_done, CR)

            def dtu_of_pair(at, s, chunks):
                kind, c = TABLE[s]
                d = int(kind[-1])
                pool.wait_ge(dt_done, at.seq(d) * 4 + (d * PAIRS + c // 2 + 1))
                for q in chunks:
                    pool.tensor_tensor(dtu[d][:, q], dt[d][:, q], u[d][:, q, PAD:], ALU.mult).then_inc(dtu_done, 1)

            pro = At("pro", None, pool)
            for s in PRO:
                if TABLE[s] in (("dt0", 1), ("dt0", 3)):
                    dtu_of_pair(pro, s, (TABLE[s][1] - 1, TABLE[s][1]))
            with pool.Fori(0, B, 1) as b:
                at = At("loop", b, pool)
                t0 = pool.snap(b * TILES)
                t0_half = pool.snap(b * (TILES // 2))

                def inputs(t):
                    d, c, i = dir_of(t), chunk_of(t), t // 2
                    if t % (TILES // NDIR) == 0:
                        pool.wait_ge(dtu_done, b * 8 + (d + 1) * KI)
                    k = RING[i]
                    loaded = (b_loaded if t % 2 == 0 else c_loaded)[k]
                    pool.wait_ge(loaded, b * (RING.count(k) * 16) + (RING[:i].count(k) + 1) * 16)
                    pool.wait_ge(scan_done, t0 + (t - 3 + CR))
                    pool.tensor_tensor(g_ring[:, t % 4], dtu[d][:, c], b_ring[:, k], ALU.mult).then_inc(g_done, 1)

                inputs(0)
                inputs(1)
                for t in range(TILES):
                    if t + 2 < TILES:
                        inputs(t + 2)
                    if t % 2 == 1:
                        pool.wait_ge(z_done, t0 + (t + 1 + CR))
                        pool.tensor_tensor(v_ring[:, t % VR], z_ring[:, t // 2 % 3], c_ring[:, RING[t // 2]],
                                           ALU.mult).then_inc(v_odd, 1)
                    for lag in (8, 9):
                        for s in slots_at(t - lag, ("dt0", "dt1")):
                            if TABLE[s][1] % 2 == 1:
                                dtu_of_pair(at, s, (TABLE[s][1] - 9 + lag,))

        @block.scalar
        def _(act):
            act.wait_ge(w_loaded, 16 * NW)
            act.activation(a_neg[:], a_neg[:], ACT.Exp).then_inc(a_exp_done, 1)
            for k in range(KM):
                for h in range(2):
                    act.wait_ge(seT_ps, k * 2 + h + 1)
                    act.activation(seT[:, k, h * HS:(h + 1) * HS], side[:, h], ACT.Copy).then_inc(seT_done, 1)
            act.wait_ge(const_done, 1)

            def side_step(at, s, lag):
                kind, i = TABLE[s]
                src, free = side[:, at.bank(s)], side_free[at.bank(s)]
                d = int(kind[-1]) if kind[-1] in "01" else None
                if lag == 2 and kind not in ("out", "cols"):
                    act.wait_ge(side_done, at.done(s))
                    if kind == "in0":
                        act.activation(xf_pad[:, i, PAD:], src, ACT.Copy).then_inc(free, 1)
                    elif kind == "res":
                        act.activation(res_gate[:, i], src, ACT.Copy, scale=0.5)
                        act.activation(res_tanh[:, i], src, ACT.Tanh, scale=0.5).then_inc(free, 1)
                    elif kind in ("conv0", "conv1"):
                        bias = b_conv_half[:, d, i:i + 1]
                        act.activation(u[d][:, i, PAD:], src, ACT.Identity, scale=0.5, bias=bias)
                        act.activation(conv_tanh[d][:, i], src, ACT.Tanh, scale=0.5, bias=bias).then_inc(free, 1)
                    elif kind in ("x0", "x1"):
                        if at.mode == "loop":
                            act.wait_ge(bc_stored, at.b * 32 + (2 - d) * 16)
                        act.activation(xdbl[0:R + N], src[0:R + N], ACT.Copy)
                        c_rows = src[R + N:R + 2 * N]
                        act.activation(xdbl[R + N:R + 2 * N], c_rows if d == 0 else c_rows[:, ::-1], ACT.Copy,
                                       scale=0.5).then_inc(free, 1)
                    elif kind in ("dt0", "dt1"):
                        bias = b_dt[:, d, i:i + 1]
                        if d == 1:
                            act.wait_ge(gate_done, at.seq(1) * KI + (i + 1))
                        act.activation(dt[d][:, i], src, ACT.Identity, bias=bias)
                        act.activation(sp_exp[d][:, i], src, ACT.Abs, bias=bias).then_inc(free, 1)
                    elif kind == "xnT":
                        act.activation(xnT[:, i], src, ACT.Identity, scale=g_col[:, i:i + 1],
                                       bias=b_col[:, i:i + 1]).then_inc(free, 1)
                    elif kind == "rows":
                        act.activation(row_t[:, i % 2 * HS:(i % 2 + 1) * HS], src, ACT.Copy).then_inc(free, 1)
                    elif kind == "rowsT":
                        act.wait_ge(rowT_stored[i % 2], at.seq(1) * 64 + (i // 2 + 1) * 16)
                        act.activation(rowT_ring[:, i % 2], src, ACT.Copy).then_inc(free, 1)
                    elif kind == "colsT":
                        act.activation(dispT_ring[:, i % 2], src, ACT.Copy).then_inc(free, 1)
                    elif kind == "slots":
                        act.wait_ge(sT_stored[i % 2], at.seq(1) * (64 * KM) + (i // 2 + 1) * (16 * KM))
                        for k in range(KM):
                            ins = act.activation(sT_ring[:, i % 2, k], src[:, k * P:(k + 1) * P], ACT.Identity,
                                                 scale=g_col[:, k:k + 1], bias=b_col[:, k:k + 1])
                        ins.then_inc(free, 1)
                if kind in ("dt0", "dt1"):
                    count = at.seq(d) * 8 + (d * KI + i + 1)
                    if lag == 3:
                        act.wait_ge(free, at.freed(s))
                        act.activation(sp_exp[d][:, i], sp_exp[d][:, i], ACT.Exp, scale=-1.0).then_inc(exp_done, 1)
                    if lag == 6 and i % 2 == 1:
                        act.wait_ge(fix_done, count)
                        act.activation(sp_one[d][:, i - 1:i + 1], sp_one[d][:, i - 1:i + 1], ACT.Ln).then_inc(ln_done, 1)
                if kind == "rows" and i % 2 == 1 and lag == 4:
                    t = i // 2
                    act.wait_ge(rmax_done, at.seq(1) * LT + (t + 1))
                    act.activation(row_t[:], row_t[:], ACT.Exp, bias=row_max[:, t:t + 1],
                                   accum_out=row_sum[:, t:t + 1]).then_inc(prob_done, 1)
                if kind == "cols" and lag == 3:
                    act.wait_ge(cmax_done, at.seq(1) * ST + (i + 1))
                    act.activation(disp_ring[:, i % 2], src, ACT.Exp, bias=col_max[:, i:i + 1],
                                   accum_out=col_sum[:, i:i + 1]).then_inc(free, 1)

            pro = At("pro", None, act)
            for s in PRO:
                for lag in range(2, 10):
                    side_step(pro, s, lag)
            with act.Fori(0, B, 1) as b:
                at = At("loop", b, act)
                t0 = act.snap(b * TILES)
                t0_half = act.snap(b * (TILES // 2))
                seq4 = act.snap(b * 4)

                def decay(t):
                    d, c, n = dir_of(t), chunk_of(t), state_of(t)
                    if t % (TILES // NDIR) == 0:
                        act.wait_ge(dt_done, seq4 + (d + 1) * PAIRS)
                    act.wait_ge(scan_done, t0 + (t - 1 + CR))
                    act.activation(e_ps[:, t % 2], dt[d][:, c], ACT.Exp, scale=a_neg[:, d, c, n:n + 1])

                decay(0)
                for t in range(TILES):
                    d, c, n = dir_of(t), chunk_of(t), state_of(t)
                    if t + 1 < TILES:
                        decay(t + 1)
                    if t % (TILES // NDIR) == 0:
                        act.wait_ge(rsum_done, b * 8 + (d + 1) * KI)
                    if t % 2 == 0:
                        act.wait_ge(v_even, t0_half + (t // 2 + CR))
                    else:
                        act.wait_ge(z_done, t0 + (t - 1 + CR))
                    act.activation(f_ps[:, t % 2], rsum[d][:, c], ACT.Tanh,
                                   scale=a_neg_half[:, d, c, n:n + 1], bias=guard_bias[:]).then_inc(f_ready, 1)
                    for s in range(SLOTS):
                        side_step(at, s, t - tile_of[s])
            epi = At("epi", None, act)
            for s in EPI:
                for lag in range(2, 10):
                    side_step(epi, s, lag)

        @block.vector
        def _(dve):
            dve.memset(guard_bias[:], HALF_NEG_LN_EPS)
            dve.memset(one[:], 1.0)
            for pad in u:
                dve.memset(pad[:, :, 0:PAD], 0.0)
            dve.memset(yg[:], 0.0)
            dve.memset(res_gate[:], 0.0)
            dve.memset(y_ps[:], 0.0).then_inc(init_done, 1)
            for sem_, n in ((side_free[0], CR), (side_free[1], CR), (scan_done, CR), (z_done, CR), (v_even, CR),
                            (x1_done, CR), (xn_normed, CR), (rinv_done, CR)):
                dve.sem_inc(sem_, n)
            dve.wait_ge(init_done, 1)
            dve.wait_ge(w_loaded, 16 * NW)
            dve.wait_ge(ident_done, 2)
            links = [0]

            def link(ins):
                links[0] += 1
                ins.then_inc(chain, 1)
                dve.wait_ge(chain, links[0])

            norm_steps(dve, link, se, se, se_stats, se_mv, se_rstd, se_tmp, se_normed)
            dve.wait_ge(se_normed, 1)
            for t in range(ST):
                ins = dve.tensor_tensor(se[:, t], se[:, t], sg_bc, ALU.mult)
            link(ins)
            for t in range(ST):
                ins = dve.tensor_tensor(se[:, t], se[:, t], sb_bc, ALU.add)
            link(ins)
            dve.tensor_scalar(se, se, scale_bc, None, ALU.mult).then_inc(se_done, 1)
            LINKS0 = links[0]
            dve.tensor_scalar(b_conv_half[:], b_conv_half[:], 0.5, None, ALU.mult)
            for d in range(NDIR):
                for c in range(KI):
                    dve.tensor_scalar(d_diag[:, d, c], ident[:], d_skip[:, d, c:c + 1], None, ALU.mult)
                    for k in range(KC):
                        dve.tensor_scalar(conv_diag[:, d, c, k], ident[:], w_conv[:, d, c, k:k + 1], None, ALU.mult)
            dve.wait_ge(a_exp_done, 1)
            dve.tensor_scalar(a_neg_half[:], a_neg[:], -0.5, None, ALU.mult).then_inc(init_done, 1)
            dve.wait_ge(init_done, 2)
            dve.tensor_scalar(a_neg[:], a_neg[:], -1.0, None, ALU.mult).then_inc(const_done, 1)
            dve.wait_ge(const_done, 1)

            def side_step(at, s, lag):
                kind, i = TABLE[s]
                src, free = side[:, at.bank(s)], side_free[at.bank(s)]
                if kind == "out" and lag == 2:
                    if i == 0:
                        dve.wait_ge(x_loaded, at.seq(1) * 16 + 16)
                    dve.wait_ge(side_done, at.done(s))
                    dve.tensor_tensor(x1[:, i], src[:, 0:DM], x1[:, i], ALU.add).then_inc(free, 1)
                if kind == "res" and lag == 4:
                    dve.wait_ge(free, at.freed(s))
                    dve.scalar_tensor_tensor(out=res_gate[:, i], in0=res_tanh[:, i], scalar=1.0, in1=res_gate[:, i],
                                             op0=ALU.add, op1=ALU.mult).then_inc(gate_done, 1)
                if kind in ("conv0", "conv1") and lag == 4:
                    d = int(kind[-1])
                    dve.wait_ge(free, at.freed(s))
                    dve.scalar_tensor_tensor(out=u[d][:, i, PAD:], in0=conv_tanh[d][:, i], scalar=1.0,
                                             in1=u[d][:, i, PAD:], op0=ALU.add, op1=ALU.mult).then_inc(u_done[d], 1)
                if kind in ("dt0", "dt1"):
                    d = int(kind[-1])
                    count = at.seq(d) * 8 + (d * KI + i + 1)
                    pairs = at.seq(d) * 4 + (d * PAIRS + i // 2 + 1)
                    dt_c, exp_c, one_c = dt[d][:, i], sp_exp[d][:, i], sp_one[d][:, i]
                    if lag == 4:
                        dve.wait_ge(exp_done, count)
                        dve.tensor_scalar(one_c, exp_c, 1.0, None, ALU.add).then_inc(one_done, 1)
                    if lag == 5:
                        dve.wait_ge(one_done, count)
                        dve.scalar_tensor_tensor(out=exp_c, in0=one_c, scalar=1.0, in1=exp_c,
                                                 op0=ALU.subtract, op1=ALU.subtract).then_inc(fix_done, 1)
                    if lag == 6:
                        dve.wait_ge(fix_done, count)
                        dve.scalar_tensor_tensor(out=dt_c, in0=dt_c, scalar=0.0, in1=exp_c,
                                                 op0=ALU.max, op1=ALU.subtract).then_inc(max_done, 1)
                    if lag == 7 and i % 2 == 1:
                        dve.wait_ge(max_done, count)
                        dve.wait_ge(ln_done, pairs)
                        dve.tensor_tensor(dt[d][:, i - 1:i + 1], dt[d][:, i - 1:i + 1], sp_one[d][:, i - 1:i + 1],
                                          ALU.add).then_inc(dt_done, 1)
                    if lag in (8, 9) and i % 2 == 1:
                        dve.wait_ge(dt_done, pairs)
                        c = i - 9 + lag
                        rsum_c, dt_c = rsum[d][:, c], dt[d][:, c]
                        dve.memset(rsum_c[:, L - 1:L] if d == 0 else rsum_c[:, 0:1], 0.0)
                        out, data = (rsum_c[:, 0:L - 1], dt_c[:, 1:L]) if d == 0 else (rsum_c[:, 1:L], dt_c[:, 0:L - 1])
                        if d == 0:
                            out, data = out[:, ::-1], data[:, ::-1]
                        dve.tensor_tensor_scan(out, one[:].broadcast_to([P, L - 1]), data, 0.0,
                                               ALU.mult, ALU.add).then_inc(rsum_done, 1)
                if kind == "rows" and i % 2 == 1:
                    if lag == 3:
                        dve.wait_ge(free, at.freed(s))
                        dve.tensor_reduce(row_max[:, i // 2:i // 2 + 1], row_t[:], AX_X, ALU.max,
                                          negate=True).then_inc(rmax_done, 1)
                    if lag == 5 and i // 2 == LT - 1:
                        dve.wait_ge(prob_done, at.seq(1) * LT + LT)
                        dve.wait_ge(rinv_stored, at.seq(1) * 16 + 16)
                        dve.reciprocal(row_inv[:], row_sum[:]).then_inc(rinv_done, 1)
                if kind == "cols":
                    if lag == 2:
                        dve.wait_ge(side_done, at.done(s))
                        dve.tensor_reduce(col_max[:, i:i + 1], src, AX_X, ALU.max, negate=True).then_inc(cmax_done, 1)
                    if lag == 4:
                        dve.wait_ge(free, at.freed(s))
                        dve.reciprocal(col_inv[:, i:i + 1], col_sum[:, i:i + 1]).then_inc(cinv_done, 1)
                    if lag == 5:
                        dve.wait_ge(cinv_done, at.seq(1) * ST + (i + 1))
                        dve.tensor_scalar(disp_ring[:, i % 2], disp_ring[:, i % 2], col_inv[:, i:i + 1], None,
                                          ALU.mult).then_inc(disp_done, 1)

            def norm_part(at, k):
                before = at.seq(1) * (2 * NORM_LINKS) + LINKS0
                if k == 0:
                    s = TABLE.index(("out", LT - 1))
                    dve.wait_ge(side_free[at.bank(s)], at.freed(s))
                elif k == NORM_STEPS:
                    dve.wait_ge(x1_done, at.seq(1) + (1 + CR))
                else:
                    dve.wait_ge(chain, before + (k if k < NORM_STEPS else k - 1))
                norm_step(dve, k % NORM_STEPS, lambda ins: ins.then_inc(chain, 1),
                          x1, x1 if k < NORM_STEPS else xn, stats, mv, rstd, tmp, x1_done if k < NORM_STEPS else xn_normed)

            def y_out(at, part):
                pair = slice(0, 2) if part in (1, 3) else slice(2, 4)
                if part in (1, 2):
                    dve.tensor_copy(yg[:, pair], y_ps[:]).then_inc(y_evac, 1)
                else:
                    dve.tensor_tensor(yg[:, pair], y_ps[:], yg[:, pair], ALU.add).then_inc(y_evac, 1)

            def y_gate(at, part):
                pair = slice(0, 2) if part == 3 else slice(2, 4)
                dve.wait_ge(y_evac, at.seq(1) * 4 + (part + 1))
                dve.tensor_tensor(yg[:, pair], yg[:, pair], res_gate[:, pair], ALU.mult).then_inc(yg_done, 1)

            pro = At("pro", None, dve)
            for s in PRO:
                for lag in range(2, 10):
                    side_step(pro, s, lag)
            with dve.Fori(0, B, 1) as b:
                at = At("loop", b, dve)
                t0 = dve.snap(b * TILES)

                def norms(t, j):
                    k = (t - NORM_TILE) * 2 + j
                    if 0 <= k < 2 * NORM_STEPS:
                        norm_part(at, k)

                def scan(t):
                    flip = (lambda ap: ap) if dir_of(t) == 0 else (lambda ap: ap[:, ::-1])
                    dve.wait_ge(f_ready, t0 + max(t, 1))
                    dve.wait_ge(g_done, t0 + (t + 1 + CR))
                    if t == 0:
                        dve.wait_ge(z_done, t0 + CR)
                    dve.tensor_tensor_scan(flip(s_ring[:, t % 3]), flip(e_ps[:, t % 2]), flip(g_ring[:, t % 4]), 0.0,
                                           ALU.mult, ALU.add).then_inc(scan_done, 1)

                def guard(t):
                    z = f_ps[:, 0] if t % 2 == 0 else z_ring[:, t // 2 % 3]
                    dve.wait_ge(f_ready, t0 + (t + 1))
                    dve.wait_ge(scan_done, t0 + (t + 1 + CR))
                    dve.scalar_tensor_tensor(out=z, in0=f_ps[:, t % 2], scalar=1.0, in1=s_ring[:, t % 3],
                                             op0=ALU.add, op1=ALU.mult).then_inc(z_done, 1)

                def times_c(t):
                    dve.wait_ge(z_done, t0 + (t + 1 + CR))
                    dve.wait_ge(v_used, t0 + ((t - VR + 2 if t else 0) + CR))
                    dve.tensor_tensor(v_ring[:, t % VR], f_ps[:, 0], c_ring[:, RING[t // 2]], ALU.mult).then_inc(v_even, 1)

                scan(0)
                for t in range(TILES):
                    part = t // SEG
                    if t % SEG == 2:
                        dve.wait_ge(v_used, t0 + (t - 2 + CR))
                        y_out(at, part)
                    if t % SEG == 3 and part in (0, 3):
                        y_gate(at, part)
                    norms(t, 0)
                    guard(t)
                    if t + 1 < TILES:
                        scan(t + 1)
                    if t % 2 == 0:
                        times_c(t)
                    norms(t, 1)
                    for s in range(SLOTS):
                        side_step(at, s, t - tile_of[s])
            epi = At("epi", None, dve)
            dve.wait_ge(v_used, B * TILES + CR)
            y_out(epi, 0)
            y_gate(epi, 0)
            for s in EPI:
                if TABLE[s] == ("xnT", 0):
                    for k in range(2 * NORM_STEPS):
                        norm_part(epi, k)
                for lag in range(2, 10):
                    side_step(epi, s, lag)

        @block.tensor
        def _(pe):
            pe.wait_ge(ident_done, 2)
            pe.wait_ge(se_done, 1)
            for k in range(KM):
                for h in range(2):
                    if k > 0:
                        pe.wait_ge(seT_done, h + 1)
                    for t in range(4):
                        mm = pe.transpose(side[:, h, t * P:(t + 1) * P], se[:, h * 4 + t, k * P:(k + 1) * P], ident[:])
                    mm.then_inc(seT_ps, 1)
            pe.wait_ge(seT_done, 4)
            pe.wait_ge(const_done, 1)
            pe.sem_inc(v_used, CR)

            def fill(at, s):
                kind, i = TABLE[s]
                bank = side[:, at.bank(s)]

                def read(kind, i):
                    other = TABLE.index((kind, i))
                    if at.bank(other) != at.bank(s):
                        pe.wait_ge(side_free[at.bank(other)], at.freed(other))

                pe.wait_ge(side_free[at.bank(s)], at.freed(s, 0))
                if kind in ("in0", "res"):
                    if kind == "in0" and i == 0:
                        pe.wait_ge(xT_loaded, at.seq(0) * 16 + 16)
                    m = i if kind == "in0" else KI + i
                    for k in range(KM):
                        mm = pe.matmul(bank, w_in[:, k, m * P:(m + 1) * P], xT_t[:, k], start=(k == 0), stop=(k == KM - 1))
                elif kind in ("conv0", "conv1"):
                    d = int(kind[-1])
                    if d == 0:
                        read("in0", i)
                    src = (xf_pad, u[0])[d]
                    for k in range(KC):
                        mm = pe.matmul(bank, conv_diag[:, d, i, k], src[:, i, k:k + L], start=(k == 0), stop=(k == KC - 1))
                elif kind in ("x0", "x1"):
                    d = int(kind[-1])
                    pe.wait_ge(u_done[d], at.seq(d) * KI + KI)
                    for c in range(KI):
                        mm = pe.matmul(bank[0:R + 2 * N], w_x[:, d, c], u[d][:, c, PAD:], start=(c == 0), stop=(c == KI - 1))
                elif kind in ("dt0", "dt1"):
                    d = int(kind[-1])
                    if i == 0:
                        read(f"x{d}", 0)
                    mm = pe.matmul(bank, w_dt[:, d, i * P:(i + 1) * P], xdbl[0:R], start=True, stop=True)
                elif kind == "out":
                    if i == 0:
                        pe.wait_ge(yg_done, at.seq(1) * 2 + 1)
                    for c in range(KI):
                        mm = pe.matmul(bank[:, 0:DM], yg[:, c, i * P:(i + 1) * P], w_out[:, c], start=(c == 0), stop=(c == KI - 1))
                elif kind == "xnT":
                    if i == 0:
                        pe.wait_ge(xn_normed, at.seq(1) + (1 + CR))
                    for t in range(LT):
                        mm = pe.transpose(bank[:, t * P:(t + 1) * P], xn[:, t, i * P:(i + 1) * P], ident[:])
                elif kind == "rows":
                    if i == 0:
                        for k in range(KM):
                            read("xnT", k)
                    t, h = i // 2, i % 2
                    for k in range(KM):
                        mm = pe.matmul(bank, xnT[:, k, t * P:(t + 1) * P], seT[:, k, h * HS:(h + 1) * HS],
                                       start=(k == 0), stop=(k == KM - 1))
                elif kind == "cols":
                    for k in range(KM):
                        mm = pe.matmul(bank, seT[:, k, i * P:(i + 1) * P], xnT[:, k], start=(k == 0), stop=(k == KM - 1))
                elif kind == "rowsT":
                    pe.wait_ge(prob_done, at.seq(1) * LT + (i // 2 + 1))
                    for c in range(4):
                        col = (i % 2 * 4 + c) * P
                        mm = pe.transpose(bank[:, c * P:(c + 1) * P], row_t[:, col:col + P], ident[:])
                elif kind == "colsT":
                    pe.wait_ge(disp_done, at.seq(1) * ST + (i + 1))
                    for t in range(LT):
                        mm = pe.transpose(bank[:, t * P:(t + 1) * P], disp_ring[:, i % 2, t * P:(t + 1) * P], ident[:])
                elif kind == "slots":
                    read("colsT", i)
                    for k in range(KM):
                        for t in range(LT):
                            mm = pe.matmul(bank[:, k * P:(k + 1) * P], xn[:, t, k * P:(k + 1) * P],
                                           dispT_ring[:, i % 2, t * P:(t + 1) * P], start=(t == 0), stop=(t == LT - 1))
                mm.then_inc(side_done, 1)

            pro = At("pro", None, pe)
            for s in PRO:
                fill(pro, s)
            with pe.Fori(0, B, 1) as b:
                at = At("loop", b, pe)
                t0_half = pe.snap(b * (TILES // 2))
                for turn in range(TILES + 2):
                    t = turn - 2
                    if t >= 0:
                        if t % SEG == 0:
                            pe.wait_ge(y_evac, b * 4 + (t // SEG + 1))
                        if t % 2 == 0:
                            pe.wait_ge(v_even, t0_half + (t // 2 + 1 + CR))
                        else:
                            pe.wait_ge(v_odd, t0_half + (t // 2 + 1 + CR))
                        pe.matmul(y_ps[:, t % 2], ident[:], v_ring[:, t % VR], start=(state_of(t) == 0), stop=True,
                                  skip_group_check=True).then_inc(v_used, 1)
                    for d, q, pair in SKIPS.get(t, ()):
                        pe.matmul(y_ps[:, q], d_diag[:, d, 2 * pair + q], u[d][:, 2 * pair + q, PAD:],
                                  start=False, stop=True, skip_group_check=True)
                    for s in range(SLOTS):
                        if tile_of[s] == turn:
                            fill(at, s)
            epi = At("epi", None, pe)
            for s in EPI:
                fill(epi, s)


def expert_stage(nc, sT_scr, Wg, bg, Wu, bu, Wd, bd, eo_scr):
    E, KM, _, ROWS = sT_scr.shape
    F, DO = Wd.shape[1:]
    B = eo_scr.shape[0]
    SE = ROWS // (B + 1)
    ROWS = B * SE
    KF = F // P
    NT = min(512, ROWS)
    HALVES, RT = ROWS // NT, ROWS // P
    UNITS = HALVES * KF
    NB = P // SE

    with ExitStack() as ctx:
        def sb(name, shape):
            return ctx.enter_context(nc.sbuf_tensor(name, shape, F32))

        def sem(name):
            return ctx.enter_context(nc.semaphore("x_" + name))

        gate_ps = ctx.enter_context(nc.psum_tensor("x_gate", [P, 2, 512], F32))
        up_ps = ctx.enter_context(nc.psum_tensor("x_up", [P, 2, 512], F32))
        down_ps = ctx.enter_context(nc.psum_tensor("x_down", [P, 4, 512], F32))
        wg = [sb(f"x_wg{q}", [P, KM, F]) for q in range(2)]
        wu = [sb(f"x_wu{q}", [P, KM, F]) for q in range(2)]
        wd = [sb(f"x_wd{q}", [P, KF, DO]) for q in range(2)]
        bd_bc = [sb(f"x_bd{q}", [P, DO]) for q in range(2)]
        xT = [sb(f"x_xT{q}", [P, KM, ROWS]) for q in range(2)]
        bg_t = [sb(f"x_bg{q}", [P, KF]) for q in range(2)]
        bu_t = [sb(f"x_bu{q}", [P, KF]) for q in range(2)]
        act_t = sb("x_act", [P, 4, NT])
        hT = [sb(f"x_hT{q}", [P, KF, ROWS]) for q in range(2)]
        eo = [sb(f"x_eo{q}", [P, RT, DO]) for q in range(2)]

        in_loaded = [sem(f"in_loaded{q}") for q in range(2)]
        gate_done, up_done, act_done, h_done = sem("gate_done"), sem("up_done"), sem("act_done"), sem("h_done")
        down_done, eo_done = sem("down_done"), sem("eo_done")
        eo_stored = [sem(f"eo_stored{q}") for q in range(2)]
        LOADS = 7

        block = ctx.enter_context(nc.Block())

        @block.sync
        def _(sp):

            def load(e, q):
                one = bass.ds(e, 1)
                sp.wait_ge(eo_done, e * RT)
                sp.dma_start(xT[q][:], sT_scr[one, :, :, SE:].rearrange("o k p r -> p (o k) r")).then_inc(in_loaded[q], 16)
                sp.dma_start(wg[q][:], Wg[one].rearrange("o (k p) f -> p (o k) f", p=P)).then_inc(in_loaded[q], 16)
                sp.dma_start(wu[q][:], Wu[one].rearrange("o (k p) f -> p (o k) f", p=P)).then_inc(in_loaded[q], 16)
                sp.dma_start(wd[q][:], Wd[one].rearrange("o (k p) f -> p (o k) f", p=P)).then_inc(in_loaded[q], 16)
                sp.dma_start(bd_bc[q][:], bd[one].broadcast_to([P, DO])).then_inc(in_loaded[q], 16)
                sp.dma_start(bg_t[q][:], bg[one].rearrange("o p k -> (o p) k")).then_inc(in_loaded[q], 16)
                sp.dma_start(bu_t[q][:], bu[one].rearrange("o p k -> (o p) k")).then_inc(in_loaded[q], 16)

            def store(e, q):
                sp.wait_ge(eo_done, (e + 2) * RT)
                for n in range(NB):
                    dst = eo_scr.rearrange("(t n) (e s) o -> e n s t o", n=NB, s=SE)[bass.ds(e, 1), n]
                    sp.dma_start(dst.rearrange("e s t o -> (e s) t o"),
                                 eo[q][n * SE:(n + 1) * SE]).then_inc(eo_stored[q], 16)

            for q in range(2):
                sp.sem_inc(eo_stored[q], NB * 16)
            load(0, 0)
            with sp.Fori(0, E - 2, 2) as e:
                load(e + 1, 1)
                store(e, 0)
                load(e + 2, 0)
                store(e + 1, 1)
            load(E - 1, 1)
            store(E - 2, 0)
            store(E - 1, 1)
            for q in range(2):
                sp.wait_ge(eo_stored[q], (E // 2 + 1) * NB * 16)

        @block.scalar
        def _(act):
            with act.Fori(0, E // 2, 1) as e2:
                for q in range(2):
                    for i in range(UNITS):
                        c, done = i % KF, q * UNITS + i + 1
                        act.wait_ge(gate_done, e2 * (2 * UNITS) + done)
                        act.wait_ge(h_done, e2 * (2 * UNITS) + done)
                        act.activation(act_t[:, i % 4], gate_ps[:, i % 2, 0:NT], ACT.Gelu,
                                       bias=bg_t[q][:, c:c + 1]).then_inc(act_done, 1)

        @block.vector
        def _(dve):
            dve.sem_inc(h_done, 4)
            dve.sem_inc(eo_done, RT)
            with dve.Fori(0, E // 2, 1) as e2:
                for q in range(2):
                    dve.wait_ge(in_loaded[q], (e2 + 1) * (LOADS * 16))
                    for i in range(UNITS):
                        c, r, done = i % KF, i // KF, q * UNITS + i + 1
                        dve.wait_ge(up_done, e2 * (2 * UNITS) + done)
                        dve.wait_ge(act_done, e2 * (2 * UNITS) + done)
                        dve.scalar_tensor_tensor(out=hT[q][:, c, r * NT:(r + 1) * NT], in0=up_ps[:, i % 2, 0:NT],
                                                 scalar=bu_t[q][:, c:c + 1],
                                                 in1=act_t[:, i % 4], op0=ALU.add, op1=ALU.mult).then_inc(h_done, 1)
                    dve.wait_ge(eo_stored[q], (e2 + 1) * (NB * 16))
                    for t in range(RT):
                        dve.wait_ge(down_done, e2 * (2 * RT) + (q * RT + t + 1))
                        dve.tensor_tensor(eo[q][:, t], down_ps[:, t % 4, 0:DO], bd_bc[q][:], ALU.add).then_inc(eo_done, 1)

        @block.tensor
        def _(pe):
            with pe.Fori(0, E // 2, 1) as e2:
                for q in range(2):
                    pe.wait_ge(in_loaded[q], (e2 + 1) * (LOADS * 16))
                    for i in range(UNITS):
                        c, r, done = i % KF, i // KF, q * UNITS + i + 1
                        pe.wait_ge(h_done, e2 * (2 * UNITS) + (done + 2))
                        for k in range(KM):
                            mm = pe.matmul(gate_ps[:, i % 2, 0:NT], wg[q][:, k, c * P:(c + 1) * P],
                                           xT[q][:, k, r * NT:(r + 1) * NT], start=(k == 0), stop=(k == KM - 1))
                        mm.then_inc(gate_done, 1)
                        for k in range(KM):
                            mm = pe.matmul(up_ps[:, i % 2, 0:NT], wu[q][:, k, c * P:(c + 1) * P],
                                           xT[q][:, k, r * NT:(r + 1) * NT], start=(k == 0), stop=(k == KM - 1))
                        mm.then_inc(up_done, 1)
                    for t in range(RT):
                        half = t * P // NT + 1
                        pe.wait_ge(h_done, e2 * (2 * UNITS) + (q * UNITS + half * KF + 4))
                        pe.wait_ge(eo_done, e2 * (2 * RT) + (q * RT + t - 3 + RT))
                        for c in range(KF):
                            mm = pe.matmul(down_ps[:, t % 4, 0:DO], hT[q][:, c, t * P:(t + 1) * P], wd[q][:, c],
                                           start=(c == 0), stop=(c == KF - 1))
                        mm.then_inc(down_done, 1)


def merge_stage(nc, pT_scr, rinv_scr, x1_scr, eo_scr, out):
    _, _, ST, L = pT_scr.shape
    B, _, DM = out.shape
    LT = L // P

    with ExitStack() as ctx:
        def sb(name, shape):
            return ctx.enter_context(nc.sbuf_tensor(name, shape, F32))

        def sem(name):
            return ctx.enter_context(nc.semaphore("m_" + name))

        acc = ctx.enter_context(nc.psum_tensor("m_acc", [P, 2, LT, 512], F32))
        pT = [sb(f"m_pT{q}", [P, ST, L]) for q in range(2)]
        eo = [sb(f"m_eo{q}", [P, ST, DM]) for q in range(2)]
        x1 = [sb(f"m_x1{q}", [P, LT, DM]) for q in range(2)]
        rinv = [sb(f"m_rinv{q}", [P, LT]) for q in range(2)]
        y = sb("m_y", [P, LT, DM])
        out_t = [sb(f"m_out{q}", [P, LT, DM]) for q in range(2)]
        stats, mv = sb("m_stats", [P, LT, 6]), sb("m_mv", [P, LT, 2])
        rstd, tmp = sb("m_rstd", [P, LT]), sb("m_tmp", [P, LT])

        in_loaded = [sem(f"in_loaded{q}") for q in range(2)]
        acc_done, y_done, chain, out_done = sem("acc_done"), sem("y_done"), sem("chain"), sem("out_done")
        stored = [sem(f"stored{q}") for q in range(2)]

        block = ctx.enter_context(nc.Block())

        @block.sync
        def _(sp):
            def load(b, q):
                one = bass.ds(b, 1)
                row = bass.ds(b + 1, 1)
                sp.wait_ge(out_done, b)
                sp.dma_start(pT[q][:], pT_scr[row].rearrange("o p t l -> (o p) t l")).then_inc(in_loaded[q], 16)
                sp.dma_start(eo[q][:], eo_scr[one].rearrange("o (t p) d -> p (o t) d", p=P)).then_inc(in_loaded[q], 16)
                sp.dma_start(x1[q][:], x1_scr[row].rearrange("o (t p) d -> p (o t) d", p=P)).then_inc(in_loaded[q], 16)
                sp.dma_start(rinv[q][:], rinv_scr[row].rearrange("o p t -> (o p) t")).then_inc(in_loaded[q], 16)

            def store(b, q):
                sp.wait_ge(out_done, b + 2)
                sp.dma_start(out[bass.ds(b, 1)].rearrange("o (t p) d -> p (o t) d", p=P), out_t[q][:]).then_inc(stored[q], 16)

            for q in range(2):
                sp.sem_inc(stored[q], 16)
            load(0, 0)
            if B > 2:
                with sp.Fori(0, B - 2, 2) as b:
                    load(b + 1, 1)
                    store(b, 0)
                    load(b + 2, 0)
                    store(b + 1, 1)
            load(B - 1, 1)
            store(B - 2, 0)
            store(B - 1, 1)
            for q in range(2):
                sp.wait_ge(stored[q], (B // 2 + 1) * 16)

        @block.vector
        def _(dve):
            PER = NORM_LINKS
            dve.sem_inc(out_done, 1)
            dve.sem_inc(y_done, 2 * LT)
            with dve.Fori(0, B // 2, 1) as b2:
                for q in range(2):
                    count = [q * PER]

                    def link(ins):
                        count[0] += 1
                        ins.then_inc(chain, 1)
                        dve.wait_ge(chain, b2 * (2 * PER) + count[0])

                    dve.wait_ge(out_done, b2 * 2 + (q + 1))
                    dve.wait_ge(in_loaded[q], (b2 + 1) * (4 * 16))
                    for t in range(LT):
                        i = q * LT + t + 1
                        dve.wait_ge(acc_done, b2 * (2 * LT) + i)
                        dve.scalar_tensor_tensor(out=y[:, t], in0=acc[:, q, t, 0:DM], scalar=rinv[q][:, t:t + 1],
                                                 in1=x1[q][:, t], op0=ALU.mult, op1=ALU.add).then_inc(y_done, 1)
                    dve.wait_ge(y_done, (b2 + 1) * (2 * LT) + (q + 1) * LT)
                    dve.wait_ge(stored[q], (b2 + 1) * 16)
                    norm_steps(dve, link, y, out_t[q], stats, mv, rstd, tmp, out_done)
                    assert count[0] == (q + 1) * PER

        @block.tensor
        def _(pe):
            with pe.Fori(0, B // 2, 1) as b2:
                for q in range(2):
                    pe.wait_ge(in_loaded[q], (b2 + 1) * (4 * 16))
                    pe.wait_ge(y_done, (b2 + 1) * (2 * LT))
                    for t in range(LT):
                        for s in range(ST):
                            mm = pe.matmul(acc[:, q, t, 0:DM], pT[q][:, s, t * P:(t + 1) * P], eo[q][:, s],
                                           start=(s == 0), stop=(s == ST - 1))
                        mm.then_inc(acc_done, 1)


def build(nc, a, out):
    x = a["x"]
    B, L, DM = x.shape
    N = a["A_log"].shape[-1]
    E, DM, F = a["Wg"].shape
    S = a["slots"].shape[0]
    x1 = nc.dram_tensor("x1_scr", (B + 1, L, DM), F32).ap()
    pT = nc.dram_tensor("pT_scr", (B + 1, P, S // P, L), F32).ap()
    rinv = nc.dram_tensor("rinv_scr", (B + 1, P, L // P), F32).ap()
    sT = nc.dram_tensor("sT_scr", (E, DM // P, P, (B + 1) * (S // E)), F32).ap()
    eo = nc.dram_tensor("eo_scr", (B, S, DM), F32).ap()
    bc = nc.dram_tensor("bc_scr", (B + 1, 2, 2 * N, L), F32).ap()
    sequence_stage(nc, a["x_T"], x, a["in_proj_T"], a["conv_w"], a["conv_b"], a["x_proj_T"], a["dt_proj_T"],
                   a["dt_proj_b"], a["A_log"], a["D"], a["out_proj_T"], a["slots"], a["slot_g"], a["slot_b"],
                   a["scale"], a["norm_g"], a["norm_b"], bc, x1, pT, rinv, sT)
    expert_stage(nc, sT, a["Wg"], a["bg"], a["Wu"], a["bu"], a["Wd"], a["bd"], eo)
    merge_stage(nc, pT, rinv, x1, eo, out)


def kernel(**inputs):
    import numpy as np
    import concourse.bacc as bacc
    from concourse.bass_utils import run_bass_kernel_spmd

    at = {k.split("_", 2)[2]: np.asarray(v) for k, v in inputs.items() if k.startswith("L0_attn_")}
    ff = {k.split("_", 2)[2]: np.asarray(v) for k, v in inputs.items() if k.startswith("L0_ffn_")}
    both = lambda f, g: np.stack([at[f], at[g]])

    def chunked(v):
        return np.moveaxis(v.reshape(v.shape[0], -1, P, *v.shape[2:]), 2, 0)

    data = {
        "x_T": at["x"].transpose(0, 2, 1),
        "x": at["x"],
        "in_proj_T": at["in_proj_w"].T,
        "conv_w": chunked(both("conv_w", "conv_b_w")[:, :, 0]),
        "conv_b": chunked(both("conv_b", "conv_b_b")),
        "x_proj_T": chunked(both("x_proj_w", "x_proj_b_w").transpose(0, 2, 1)),
        "dt_proj_T": both("dt_proj_w", "dt_proj_b_w").transpose(0, 2, 1),
        "dt_proj_b": chunked(both("dt_proj_b", "dt_proj_b_b")),
        "A_log": chunked(both("A_log", "A_b_log")),
        "D": chunked(both("D", "D_b")),
        "out_proj_T": at["out_proj_w"].T,
        "slots": ff["slot_embeds"].reshape(-1, ff["slot_embeds"].shape[-1]),
        "bg": chunked(ff["bg"]).swapaxes(0, 1),
        "bu": chunked(ff["bu"]).swapaxes(0, 1),
        "norm_g": ff["norm_g"].reshape(-1, P).T,
        "norm_b": ff["norm_b"].reshape(-1, P).T,
        **{n: ff[n] for n in ("slot_g", "slot_b", "scale", "Wg", "Wu", "Wd", "bd")},
    }
    nc = bacc.Bacc("TRN2", target_bir_lowering=False, num_devices=1)
    arrays, aps = {}, {}
    for name, v in data.items():
        arrays[f"in_{name}"] = np.ascontiguousarray(v)
        aps[name] = nc.dram_tensor(f"in_{name}", v.shape, mybir.dt.from_np(v.dtype), kind="ExternalInput").ap()
    out = nc.dram_tensor("out", at["x"].shape, F32, kind="ExternalOutput").ap()
    build(nc, aps, out)
    r = run_bass_kernel_spmd(nc, [arrays], core_ids=[0])
    return r.results[0]["out"]
```
